# Optimizing a Trainium2 kernel written in Bass

```python
import numpy as np
import jax
import jax.numpy as jnp

def _softmax(x, axis=-1):
    return jax.nn.softmax(x, axis=axis)

def _gelu(x):
    return jax.nn.gelu(x, approximate=True)

def _silu(x):
    return jax.nn.silu(x)

def _sigmoid(x):
    return jax.nn.sigmoid(x)

def _layernorm(x, axis=-1, eps=1e-05):
    m = jnp.mean(x, axis=axis, keepdims=True)
    v = jnp.var(x, axis=axis, keepdims=True)
    return (x - m) / jnp.sqrt(v + eps)

def _scatter_add(tgt, idx, src, axis=0):
    return tgt.at[idx].add(src)

def _segment_sum(src, seg, n):
    return jax.ops.segment_sum(src, seg, n)
kernel_name = 'mk_adj_seq_d1_adj_r2_60f6d4'

def setup_inputs(seed: int=0):
    np.random.seed(seed)
    _w = jnp.asarray

    def _rec_inputs():
        import jax
        import jax.numpy as jnp
        _gk = jax.random.key(seed)
        x = -0.0005207 + 1.001 * jax.random.normal(jax.random.fold_in(_gk, 1), (64, 128, 256), jnp.float32)
        _w = (1.0 + jnp.arange(128, dtype=jnp.float32)) ** (-0.5)
        _w = _w / _w.mean()
        _pij = jnp.clip(0.03125 * _w[:, None] * _w[None, :], 0.0, 1.0)
        _a = jax.random.uniform(jax.random.fold_in(_gk, 2), (64, 128, 128)) < _pij
        adj = _a
        return (x, adj)
    x, adj = _rec_inputs()

    def _L0_gnn_setup():
        import jax, jax.numpy as jnp
        import numpy as np
        HIDDEN = 256
        HEADS = 8
        HEAD_DIM = HIDDEN // HEADS
        D_FF = 4 * HIDDEN
        NEG = -1000000000.0

        def _layernorm(x, g, b, eps=1e-05):
            mu = jnp.mean(x, axis=-1, keepdims=True)
            var = jnp.var(x, axis=-1, keepdims=True)
            return (x - mu) * jax.lax.rsqrt(var + eps) * g + b
        key = jax.random.key(seed)
        ks = jax.random.split(key, 16)
        B, S = (2, 1024)
        s = 1.0 / np.sqrt(HIDDEN)
        inp = {'x': jax.random.normal(ks[0], (B, S, HIDDEN), dtype=jnp.float32), 'adj_mask': jax.random.bernoulli(ks[1], 0.5, (B, S, S)), 'ln1_g': jnp.ones((HIDDEN,), jnp.float32), 'ln1_b': jnp.zeros((HIDDEN,), jnp.float32), 'ln2_g': jnp.ones((HIDDEN,), jnp.float32), 'ln2_b': jnp.zeros((HIDDEN,), jnp.float32), 'Wq': jax.random.uniform(ks[2], (HIDDEN, HIDDEN), jnp.float32, -s, s), 'bq': jnp.zeros((HIDDEN,), jnp.float32), 'Wk': jax.random.uniform(ks[3], (HIDDEN, HIDDEN), jnp.float32, -s, s), 'bk': jnp.zeros((HIDDEN,), jnp.float32), 'Wv': jax.random.uniform(ks[4], (HIDDEN, HIDDEN), jnp.float32, -s, s), 'bv': jnp.zeros((HIDDEN,), jnp.float32), 'Wo': jax.random.uniform(ks[5], (HIDDEN, HIDDEN), jnp.float32, -s, s), 'bo': jnp.zeros((HIDDEN,), jnp.float32), 'W1': jax.random.uniform(ks[6], (HIDDEN, D_FF), jnp.float32, -s, s), 'b1': jnp.zeros((D_FF,), jnp.float32), 'W2': jax.random.uniform(ks[7], (D_FF, HIDDEN), jnp.float32, -1.0 / np.sqrt(D_FF), 1.0 / np.sqrt(D_FF)), 'b2': jnp.zeros((HIDDEN,), jnp.float32)}
        return inp
    _L0_gnn_all = _L0_gnn_setup()
    _L0_gnn_in = {k: v for k, v in _L0_gnn_all.items() if k in ('ln1_g', 'ln1_b', 'ln2_g', 'ln2_b', 'Wq', 'bq', 'Wk', 'bk', 'Wv', 'bv', 'Wo', 'bo', 'W1', 'b1', 'W2', 'b2')}
    del _L0_gnn_all
    return {'x': x, 'adj': adj, 'L0_gnn_ln1_g': _L0_gnn_in['ln1_g'], 'L0_gnn_ln1_b': _L0_gnn_in['ln1_b'], 'L0_gnn_ln2_g': _L0_gnn_in['ln2_g'], 'L0_gnn_ln2_b': _L0_gnn_in['ln2_b'], 'L0_gnn_Wq': _L0_gnn_in['Wq'], 'L0_gnn_bq': _L0_gnn_in['bq'], 'L0_gnn_Wk': _L0_gnn_in['Wk'], 'L0_gnn_bk': _L0_gnn_in['bk'], 'L0_gnn_Wv': _L0_gnn_in['Wv'], 'L0_gnn_bv': _L0_gnn_in['bv'], 'L0_gnn_Wo': _L0_gnn_in['Wo'], 'L0_gnn_bo': _L0_gnn_in['bo'], 'L0_gnn_W1': _L0_gnn_in['W1'], 'L0_gnn_b1': _L0_gnn_in['b1'], 'L0_gnn_W2': _L0_gnn_in['W2'], 'L0_gnn_b2': _L0_gnn_in['b2']}

def reference(x, adj, L0_gnn_ln1_g, L0_gnn_ln1_b, L0_gnn_ln2_g, L0_gnn_ln2_b, L0_gnn_Wq, L0_gnn_bq, L0_gnn_Wk, L0_gnn_bk, L0_gnn_Wv, L0_gnn_bv, L0_gnn_Wo, L0_gnn_bo, L0_gnn_W1, L0_gnn_b1, L0_gnn_W2, L0_gnn_b2):
    import jax
    import jax.numpy as jnp

    def _L0_gnn_ref(x, adj_mask, ln1_g, ln1_b, ln2_g, ln2_b, Wq, bq, Wk, bk, Wv, bv, Wo, bo, W1, b1, W2, b2):
        import jax, jax.numpy as jnp
        import numpy as np
        HIDDEN = 256
        HEADS = 8
        HEAD_DIM = HIDDEN // HEADS
        D_FF = 4 * HIDDEN
        NEG = -1000000000.0

        def _layernorm(x, g, b, eps=1e-05):
            mu = jnp.mean(x, axis=-1, keepdims=True)
            var = jnp.var(x, axis=-1, keepdims=True)
            return (x - mu) * jax.lax.rsqrt(var + eps) * g + b
        B, S, H = x.shape
        nx = _layernorm(x, ln1_g, ln1_b)
        q = (nx @ Wq + bq).reshape(B, S, HEADS, HEAD_DIM)
        k = (nx @ Wk + bk).reshape(B, S, HEADS, HEAD_DIM)
        v = (nx @ Wv + bv).reshape(B, S, HEADS, HEAD_DIM)
        scores = jnp.einsum('bqhd,bkhd->bhqk', q, k) / np.sqrt(HEAD_DIM)
        scores = jnp.where(adj_mask[:, None, :, :], scores, NEG)
        attn = jax.nn.softmax(scores, axis=-1)
        out = jnp.einsum('bhqk,bkhd->bqhd', attn, v).reshape(B, S, H)
        out = out @ Wo + bo
        x = x + out
        nx = _layernorm(x, ln2_g, ln2_b)
        mlp = jax.nn.gelu(nx @ W1 + b1, approximate=False) @ W2 + b2
        return x + mlp
    x = _L0_gnn_ref(x, adj, L0_gnn_ln1_g, L0_gnn_ln1_b, L0_gnn_ln2_g, L0_gnn_ln2_b, L0_gnn_Wq, L0_gnn_bq, L0_gnn_Wk, L0_gnn_bk, L0_gnn_Wv, L0_gnn_bv, L0_gnn_Wo, L0_gnn_bo, L0_gnn_W1, L0_gnn_b1, L0_gnn_W2, L0_gnn_b2)
    return x

_drawn_inputs = setup_inputs


def setup_inputs(seed=0):
    import zlib

    import numpy as np

    out = dict(_drawn_inputs(seed))
    spreads = {'L0_gnn_ln1_g': (1.0, 0.2),
     'L0_gnn_ln1_b': (0.0, 0.1),
     'L0_gnn_ln2_g': (1.0, 0.2),
     'L0_gnn_ln2_b': (0.0, 0.387),
     'L0_gnn_bq': (0.0, 0.8),
     'L0_gnn_bk': (0.0, 0.8),
     'L0_gnn_bv': (0.0, 0.1),
     'L0_gnn_bo': (0.0, 0.1),
     'L0_gnn_b1': (0.0, 0.1),
     'L0_gnn_b2': (0.0, 0.1)}
    factors = {}
    for name, (base, spread) in spreads.items():
        noise = np.random.default_rng([zlib.crc32(name.encode()), seed]).standard_normal(out[name].shape)
        drawn = base * np.exp(spread * noise) if base else spread * noise
        out[name] = jnp.asarray(drawn.astype(out[name].dtype))
    for name, factor in factors.items():
        out[name] = (out[name] * factor).astype(out[name].dtype)
    return out
```

```python
import concourse.bass as bass
from concourse import mybir
from contextlib import ExitStack

FP32 = mybir.dt.float32
F32R = mybir.dt.float32r
U8 = mybir.dt.uint8
ALU = mybir.AluOpType
ACT = mybir.ActivationFunctionType

P = 128
EPS = 1e-5
MASKED = 1e30


def build_gnn_layer(nc, x, adj, ln1_g, ln1_b, ln2_g, ln2_b, wq, bq, wk, bk, wv, bv, wo, bo,
                    w1, b1, w2, b2, out):
    G, S, H = x.shape
    HEADS = 8
    D = H // HEADS
    FF = w1.shape[1]
    KT = H // P
    HPT = P // D
    FT = FF // P
    PAIRS = G // 2
    T2 = 2 * S
    BG = 4
    TB = BG * S
    BLOCKS = G // BG
    SCALE = float(D) ** -0.5
    assert S == P and H == 2 * P and HPT == 4 and FT == 8

    ctx = ExitStack()
    with ctx:
        def sb(name, shape, dt=FP32):
            return ctx.enter_context(nc.sbuf_tensor(name, shape, dt))

        def sem(name):
            return ctx.enter_context(nc.semaphore(name))

        xs = sb("xs", [P, G, H])
        adj_u8 = sb("adj_u8", [P, G, S], U8)
        qkv_raw = sb("qkv_raw", [P, 3, KT, H])
        wqkv_hi = sb("wqkv_hi", [P, 3, KT, H], F32R)
        wqkv_lo = sb("wqkv_lo", [P, 3, KT, H], F32R)
        wo_sb = sb("wo_sb", [P, KT, H])
        mlp_f32 = sb("mlp_f32", [P, 2, FT * H])
        w1_hi = sb("w1_hi", [P, KT, FF], F32R)
        w1_lo = sb("w1_lo", [P, KT, FF], F32R)
        w2_hi = sb("w2_hi", [P, FT, H], F32R)
        w2_lo = sb("w2_lo", [P, FT, H], F32R)
        w1_raw = mlp_f32[:, 0, :].rearrange("p (k n) -> p k n", k=KT)
        w2_raw = mlp_f32[:, 1, :].rearrange("p (f n) -> p f n", f=FT)
        ln_cols = sb("ln_cols", [P, 4, KT])
        bias_cols = sb("bias_cols", [P, 3, KT])
        b1_cols = sb("b1_cols", [P, FT])
        qkv_bias = sb("qkv_bias", [P, 3, KT])
        mlp_bias = sb("mlp_bias", [P, FT])
        bv_wide = sb("bv_wide", [P, KT, P])
        bo_rows = sb("bo_rows", [P, H])
        b2_rows = sb("b2_rows", [P, H])
        out_bias = sb("out_bias", [P, H])
        ident = sb("ident", [P, P])
        minus_half = sb("minus_half", [P, BG])

        stats = sb("stats", [P, 2, 6])
        mv = sb("mv", [P, 2, 2])
        var_eps = sb("var_eps", [P, 2])
        rstd = sb("rstd", [P, 2])
        nx = sb("nx", [P, 2, H])
        nt_hi = sb("nt_hi", [P, KT, T2], F32R)
        nt_lo = sb("nt_lo", [P, KT, T2], F32R)
        qT = sb("qT", [P, KT, T2])
        kz = sb("kz", [P, KT, HPT, T2])
        v_sb = sb("v_sb", [P, 2, H])
        mask_add = sb("mask_add", [P, 2, S])
        z_neg = sb("z_neg", [P, HEADS, S])
        min_z = sb("min_z", [P, HEADS])
        e_sb = sb("e_sb", [P, HEADS, S])
        sums = sb("sums", [P, HEADS])
        rinv = sb("rinv", [P, HEADS])
        p_sb = sb("p_sb", [P, HEADS, S])
        pT = sb("pT", [P, HEADS, S])
        oT = sb("oT", [P, KT, S])

        stats2 = sb("stats2", [P, BG, 6])
        mv2 = sb("mv2", [P, BG, 2])
        var_eps2 = sb("var_eps2", [P, BG])
        rstd2 = sb("rstd2", [P, BG])
        nx2 = mlp_f32[:, 0, 0:BG * H].rearrange("p (g c) -> p g c", g=BG)
        h_sb = mlp_f32[:, 1, 0:2 * TB].rearrange("p (u t) -> p u t", u=2)
        n2_hi = sb("n2_hi", [P, KT, TB], F32R)
        n2_lo = sb("n2_lo", [P, KT, TB], F32R)
        h_hi = sb("h_hi", [P, 2, TB], F32R)
        h_lo = sb("h_lo", [P, 2, TB], F32R)

        bank = [ctx.enter_context(nc.psum_tensor(f"bank{n}", [P, 512], FP32)) for n in range(8)]
        tq_ps = bank[0][:, :].rearrange("p (k t) -> p k t", k=KT)
        k_ps = bank[1][:, :].rearrange("p (k t) -> p k t", k=KT)
        v_ps = bank[2][:, :].rearrange("p (g c) -> p g c", g=2)
        s_ps = [bank[3 + k][:, :].rearrange("p (h k) -> p h k", h=HPT) for k in range(KT)]
        pt_ps = [bank[5 + k][:, :].rearrange("p (h q) -> p h q", h=HPT) for k in range(KT)]
        o_ps = bank[7][:, 0:H].rearrange("p (k q) -> p k q", k=KT)
        wo_ps = bank[7][:, H:2 * H]
        t2_ps = [bank[k] for k in range(KT)]
        h_ps = [bank[2], bank[3]]
        y_ps = [bank[4 + j][:, 0:H] for j in range(BG)]

        wait_taken = sem("wait_taken")
        x_in = sem("x_in")
        adj_in = sem("adj_in")
        qkv_in = sem("qkv_in")
        small_in = sem("small_in")
        rows_in = sem("rows_in")
        wo_in = sem("wo_in")
        mlp_in = sem("mlp_in")
        out_done = sem("out_done")
        id_zero = sem("id_zero")
        consts = sem("consts")
        kz_zero = sem("kz_zero")
        w_hi = sem("w_hi")
        w_lo = sem("w_lo")
        mlp_hi = sem("mlp_hi")
        mlp_lo = sem("mlp_lo")
        bias_mm = sem("bias_mm")
        bias_done = sem("bias_done")
        bv_done = sem("bv_done")
        bo_mm = sem("bo_mm")
        bo_done = sem("bo_done")

        stats_done = sem("stats_done")
        mv_done = sem("mv_done")
        var_done = sem("var_done")
        rstd_done = sem("rstd_done")
        nx_done = sem("nx_done")
        mask_done = sem("mask_done")
        xb_done = sem("xb_done")
        t_done = sem("t_done")
        hi_done = sem("hi_done")
        lo_done = sem("lo_done")
        k_mm = sem("k_mm")
        q_mm = sem("q_mm")
        v_mm = sem("v_mm")
        k_act = sem("k_act")
        k_dve = sem("k_dve")
        q_out = sem("q_out")
        v_out = sem("v_out")
        s_mm = sem("s_mm")
        z_done = sem("z_done")
        e_done = sem("e_done")
        rinv_done = sem("rinv_done")
        p_done = sem("p_done")
        pt_mm = sem("pt_mm")
        pt_act = sem("pt_act")
        pt_dve = sem("pt_dve")
        pv_mm = sem("pv_mm")
        o_out = sem("o_out")
        wo_mm = sem("wo_mm")
        x1_done = sem("x1_done")

        stats2_done = sem("stats2_done")
        mv2_done = sem("mv2_done")
        var2_done = sem("var2_done")
        rstd2_done = sem("rstd2_done")
        nx2_done = sem("nx2_done")
        xb2_done = sem("xb2_done")
        t2_mm = sem("t2_mm")
        n2_hi_done = sem("n2_hi_done")
        n2_lo_done = sem("n2_lo_done")
        w1_mm = sem("w1_mm")
        gelu_done = sem("gelu_done")
        h_hi_done = sem("h_hi_done")
        h_lo_done = sem("h_lo_done")
        w2_mm = sem("w2_mm")
        y_out = sem("y_out")

        def wait(eng, s, value):
            if not isinstance(value, int) or value > 0:
                eng.wait_ge(s, value)

        def apart(dve):
            dve.sem_inc(wait_taken, 1)

        block = ctx.enter_context(nc.Block())

        @block.sync
        def _(sp):
            x_pairs = x.rearrange("g p c -> p g c")
            out_blocks = out.rearrange("g p c -> p g c")

            def load_pair(i):
                wait(sp, x_in, 16 * i)
                sp.dma_start(xs[:, bass.ts(i, 2), :], x_pairs[:, bass.ts(i, 2), :]).then_inc(x_in, 16)

            load_pair(0)
            sp.dma_start(adj_u8[:, :, :], adj).then_inc(adj_in, 16)
            load_pair(1)
            sp.dma_start(wo_sb[:, :, :], wo.rearrange("(k p) n -> p k n", p=P)).then_inc(wo_in, 16)
            sp.dma_start(w1_raw, w1.rearrange("(k p) n -> p k n", p=P)).then_inc(mlp_in, 16)
            sp.dma_start(w2_raw, w2.rearrange("(f p) n -> p f n", p=P)).then_inc(mlp_in, 16)
            with nc.sync.Fori(2, PAIRS) as i:
                load_pair(i)
            with nc.sync.Fori(0, BLOCKS) as t:
                sp.wait_ge(y_out, BG * t + BG)
                sp.dma_start(out_blocks[:, bass.ts(t, BG), :], xs[:, bass.ts(t, BG), :])\
                    .then_inc(out_done, 16)
            sp.wait_ge(out_done, 16 * BLOCKS)

        @block.gpsimd
        def _(pool):
            nc.gpsimd.memset(ident[:, :], 0.0).then_inc(id_zero, 1)
            pool.wait_ge(id_zero, 1)
            nc.gpsimd.affine_select(out=ident[:, :], in_=ident[:, :], compare_op=ALU.not_equal,
                                    fill=1.0, base=0, pattern=[[-1, P]], channel_multiplier=1)\
                .then_inc(consts, 1)
            nc.gpsimd.memset(minus_half[:, :], -0.5).then_inc(consts, 1)
            pool.wait_ge(consts, 2)
            for n, row in enumerate((bo, b2)):
                dst = (bo_rows, b2_rows)[n]
                nc.gpsimd.dma_start(dst[:, :], row.partition_broadcast(P)).then_inc(rows_in, 16)

            def inv_std(i):
                wait(pool, var_done, i + 1)
                wait(pool, nx_done, i)
                nc.gpsimd.tensor_tensor(rstd[:, :], var_eps[:, :], minus_half[:, 0:2], ALU.pow)\
                    .then_inc(rstd_done, 1)

            def normalise(g):
                for k in range(KT):
                    wait(pool, rinv_done, 2 * g + k + 1)
                    wait(pool, pt_mm, 2 * g)
                    hs = slice(HPT * k, HPT * k + HPT)
                    nc.gpsimd.tensor_tensor(p_sb[:, hs, :], e_sb[:, hs, :],
                                            rinv[:, hs].unsqueeze(2).to_broadcast([P, HPT, S]),
                                            ALU.mult).then_inc(p_done, 1)

            def add_out_bias(i):
                wait(pool, nx_done, i + 1)
                nc.gpsimd.tensor_tensor(xs[:, bass.ts(i, 2), :], xs[:, bass.ts(i, 2), :],
                                        out_bias[:, :].unsqueeze(1).to_broadcast([P, 2, H]),
                                        ALU.add).then_inc(xb_done, 1)

            def pair(i, ahead):
                normalise(2 * i)
                if ahead >= 2:
                    inv_std(i + 2)
                if ahead >= 1:
                    add_out_bias(i + 1)
                normalise(2 * i + 1)

            inv_std(0)
            inv_std(1)
            pool.wait_ge(bo_done, 1)
            add_out_bias(0)
            pair(0, 2)
            with nc.gpsimd.Fori(1, PAIRS - 2) as i:
                pair(i, 2)
            pair(PAIRS - 2, 1)
            pair(PAIRS - 1, 0)

            def inv_std2(t):
                wait(pool, var2_done, t + 1)
                nc.gpsimd.tensor_tensor(rstd2[:, :], var_eps2[:, :], minus_half[:, :], ALU.pow)\
                    .then_inc(rstd2_done, 1)

            def add_mlp_bias(t):
                wait(pool, nx2_done, t + 1)
                nc.gpsimd.tensor_tensor(xs[:, bass.ts(t, BG), :], xs[:, bass.ts(t, BG), :],
                                        b2_rows[:, :].unsqueeze(1).to_broadcast([P, BG, H]),
                                        ALU.add).then_inc(xb2_done, 1)

            inv_std2(0)
            add_mlp_bias(0)
            with nc.gpsimd.Fori(1, BLOCKS) as t:
                inv_std2(t)
                add_mlp_bias(t)

        @block.scalar
        def _(act):
            for n, w in enumerate((wq, wk, wv)):
                act.dma_start(qkv_raw[:, n, :, :], w.rearrange("(k p) n -> p k n", p=P))\
                    .then_inc(qkv_in, 16)
            for n, v in enumerate((ln1_g, ln1_b, ln2_g, ln2_b)):
                act.dma_start(ln_cols[:, n, :], v).then_inc(small_in, 16)
            for n, v in enumerate((bq, bk, bv)):
                act.dma_start(bias_cols[:, n, :], v).then_inc(small_in, 16)
            act.dma_start(b1_cols[:, :], b1).then_inc(small_in, 16)

            act.wait_ge(qkv_in, 48)
            act.wait_ge(small_in, 128)
            for n in range(3):
                for k in range(KT):
                    nc.scalar.activation(wqkv_hi[:, n, k, :], qkv_raw[:, n, k, :], ACT.Copy,
                                         scale=ln_cols[:, 0, k:k + 1]).then_inc(w_hi, 1)

            def upper_half(i):
                wait(act, t_done, i + 1)
                wait(act, v_mm, i)
                nc.scalar.activation(nt_hi[:, :, :], tq_ps, ACT.Copy).then_inc(hi_done, 1)

            def key_blocks(i):
                wait(act, k_mm, i + 1)
                wait(act, s_mm, 4 * i)
                wait(act, kz_zero, 1)
                for j in range(HPT // 2):
                    q = slice(D * j, D * j + D)
                    for k in range(KT):
                        last = nc.scalar.activation(kz[q, k, j, :], k_ps[q, k, :], ACT.Identity,
                                                    bias=qkv_bias[q, 1, k:k + 1])
                        last.then_inc(k_act, 1)

            def queries(i):
                wait(act, q_mm, i + 1)
                for k in range(KT):
                    nc.scalar.activation(qT[:, k, :], tq_ps[:, k, :], ACT.Identity,
                                         bias=qkv_bias[:, 0, k:k + 1]).then_inc(q_out, 1)

            def values(i):
                wait(act, v_mm, i + 1)
                wait(act, pv_mm, 2 * i)
                nc.scalar.activation(v_sb[:, :, :], v_ps, ACT.Copy).then_inc(v_out, 1)

            def exps(g, heads):
                for h in heads:
                    wait(act, z_done, HEADS * g + h + 1)
                    if h == 0:
                        wait(act, p_done, 2 * g)
                    nc.scalar.activation(e_sb[:, h, :], z_neg[:, h, :], ACT.Exp,
                                         bias=min_z[:, h:h + 1], scale=-1.0,
                                         accum_out=sums[:, h:h + 1]).then_inc(e_done, 1)

            def weights_out(g):
                wait(act, pt_mm, 2 * g + 1)
                wait(act, pv_mm, g)
                nc.scalar.activation(pT[:, 0:HPT, :], pt_ps[0], ACT.Copy).then_inc(pt_act, 1)

            def pair(i, first, last):
                exps(2 * i, range(HPT))
                if not first:
                    weights_out(2 * i - 1)
                exps(2 * i, range(HPT, HEADS))
                values(i)
                if not last:
                    upper_half(i + 1)
                exps(2 * i + 1, range(HPT))
                weights_out(2 * i)
                exps(2 * i + 1, range(HPT, HEADS))
                if not last:
                    key_blocks(i + 1)
                    queries(i + 1)

            upper_half(0)
            act.wait_ge(bias_done, 1)
            key_blocks(0)
            queries(0)
            act.wait_ge(mlp_in, 32)
            for k in range(KT):
                nc.scalar.activation(w1_hi[:, k, :], w1_raw[:, k, :], ACT.Copy,
                                     scale=ln_cols[:, 2, k:k + 1]).then_inc(mlp_hi, 1)
            nc.scalar.activation(w2_hi[:, :, :], w2_raw, ACT.Copy).then_inc(mlp_hi, 1)
            pair(0, True, False)
            with nc.scalar.Fori(1, PAIRS - 1) as i:
                pair(i, False, False)
            pair(PAIRS - 1, False, True)
            weights_out(G - 1)

            def upper_half2(t):
                for k in range(KT):
                    wait(act, t2_mm, KT * t + k + 1)
                    wait(act, w1_mm, FT * t)
                    nc.scalar.activation(n2_hi[:, k, :], t2_ps[k][:, :], ACT.Copy)\
                        .then_inc(n2_hi_done, 1)

            def gelus(t):
                for f in range(FT):
                    wait(act, w1_mm, FT * t + f + 1)
                    wait(act, h_lo_done, FT * t + f - 1)
                    nc.scalar.activation(h_sb[:, f % 2, :], h_ps[f % 2][:, :], ACT.Gelu,
                                         bias=mlp_bias[:, f:f + 1]).then_inc(gelu_done, 1)

            upper_half2(0)
            gelus(0)
            with nc.scalar.Fori(1, BLOCKS) as t:
                upper_half2(t)
                gelus(t)

        @block.vector
        def _(dve):
            nc.vector.memset(kz[:, :, :, :], 0.0).then_inc(kz_zero, 1)

            def pair_stats(i):
                wait(dve, x_in, 16 * i + 16)
                for j in range(2):
                    nc.vector.bn_stats(stats[:, j, :], xs[:, 2 * i + j, :]).then_inc(stats_done, 1)
                for j in range(2):
                    wait(dve, stats_done, 2 * i + j + 1)
                    apart(dve)
                    nc.vector.bn_aggr(mv[:, j, :], stats[:, j, :]).then_inc(mv_done, 1)
                wait(dve, mv_done, 2 * i + 2)
                wait(dve, rstd_done, i)
                nc.vector.tensor_scalar(var_eps[:, :], mv[:, :, 1], EPS, None, ALU.add)\
                    .then_inc(var_done, 1)

            def pair_norm(i):
                wait(dve, rstd_done, i + 1)
                wait(dve, t_done, i)
                for j in range(2):
                    last = nc.vector.tensor_scalar(nx[:, j, :], xs[:, 2 * i + j, :], mv[:, j, 0:1],
                                                   rstd[:, j:j + 1], ALU.subtract, ALU.mult)
                last.then_inc(nx_done, 1)

            def masks(i):
                wait(dve, z_done, 2 * HEADS * i)
                nc.vector.tensor_scalar(mask_add[:, :, :], adj_u8[:, bass.ts(i, 2), :],
                                        MASKED, MASKED, ALU.mult, ALU.subtract).then_inc(mask_done, 1)

            def scores(g, j):
                wait(dve, e_done, HEADS * g)
                for h in range(HEADS):
                    if h % HPT == 0:
                        wait(dve, s_mm, 2 * g + h // HPT + 1)
                        apart(dve)
                    nc.vector.tensor_tensor_reduce(
                        out=z_neg[:, h, :], in0=s_ps[h // HPT][:, h % HPT, :], in1=mask_add[:, j, :],
                        scale=-SCALE, scalar=3e38, op0=ALU.add, op1=ALU.min,
                        accum_out=min_z[:, h:h + 1]).then_inc(z_done, 1)

            def reciprocals(g, k):
                wait(dve, e_done, HEADS * g + HPT * (k + 1))
                hs = slice(HPT * k, HPT * k + HPT)
                nc.vector.reciprocal(rinv[:, hs], sums[:, hs]).then_inc(rinv_done, 1)

            def weights_out(g):
                wait(dve, pt_mm, 2 * g + 2)
                wait(dve, pv_mm, g)
                nc.vector.tensor_copy(pT[:, HPT:HEADS, :], pt_ps[1]).then_inc(pt_dve, 1)

            def heads_out(g):
                wait(dve, pv_mm, g + 1)
                wait(dve, wo_mm, g)
                nc.vector.tensor_copy(oT[:, :, :], o_ps).then_inc(o_out, 1)

            def residual(i, g):
                wait(dve, wo_mm, g + 1)
                wait(dve, xb_done, i + 1)
                nc.vector.tensor_tensor(xs[:, g, :], wo_ps, xs[:, g, :], ALU.add).then_inc(x1_done, 1)

            def lower_half(i):
                wait(dve, hi_done, i + 1)
                wait(dve, v_mm, i)
                nc.vector.tensor_tensor(nt_lo[:, :, :], tq_ps, nt_hi[:, :, :].bitcast(FP32), ALU.subtract)\
                    .then_inc(lo_done, 1)

            def key_blocks(i):
                wait(dve, k_mm, i + 1)
                wait(dve, s_mm, 4 * i)
                for j in range(HPT // 2, HPT):
                    q = slice(D * j, D * j + D)
                    for k in range(KT):
                        nc.vector.tensor_scalar(kz[q, k, j, :], k_ps[q, k, :],
                                                qkv_bias[q, 1, k:k + 1], None, ALU.add)\
                            .then_inc(k_dve, 1)

            dve.wait_ge(consts, 2)
            pair_stats(0)
            pair_norm(0)
            dve.wait_ge(qkv_in, 48)
            dve.wait_ge(small_in, 128)
            for n in range(3):
                for k in range(KT):
                    dve.wait_ge(w_hi, n * KT + k + 1)
                    nc.vector.scalar_tensor_tensor(
                        out=wqkv_lo[:, n, k, :], in0=qkv_raw[:, n, k, :], scalar=ln_cols[:, 0, k:k + 1],
                        in1=wqkv_hi[:, n, k, :].bitcast(FP32), op0=ALU.mult, op1=ALU.subtract).then_inc(w_lo, 1)
            dve.wait_ge(bias_mm, 1)
            bias_ps = bank[7]
            nc.vector.tensor_tensor(qkv_bias[:, :, :], bias_ps[:, 0:3 * KT].rearrange("p (n k) -> p n k", n=3),
                                    bias_cols[:, :, :], ALU.add).then_inc(bias_done, 1)
            lower_half(0)
            dve.wait_ge(bias_done, 1)
            for k in range(KT):
                last = nc.vector.tensor_scalar(bv_wide[:, k, :], ident[:, :], 0.0, qkv_bias[:, 2, k:k + 1],
                                               ALU.mult, ALU.add)
            last.then_inc(bv_done, 1)
            dve.wait_ge(kz_zero, 1)
            key_blocks(0)
            pair_stats(1)
            pair_norm(1)
            dve.wait_ge(adj_in, 16)
            masks(0)
            dve.wait_ge(rows_in, 32)
            dve.wait_ge(bo_mm, 1)
            nc.vector.tensor_tensor(out_bias[:, :], wo_ps, bo_rows[:, :], ALU.add).then_inc(bo_done, 1)
            dve.wait_ge(mlp_in, 32)
            for k in range(KT):
                dve.wait_ge(mlp_hi, k + 1)
                nc.vector.scalar_tensor_tensor(
                    out=w1_lo[:, k, :], in0=w1_raw[:, k, :], scalar=ln_cols[:, 2, k:k + 1],
                    in1=w1_hi[:, k, :].bitcast(FP32), op0=ALU.mult, op1=ALU.subtract).then_inc(mlp_lo, 1)
            dve.wait_ge(mlp_hi, KT + 1)
            nc.vector.tensor_tensor(w2_lo[:, :, :], w2_raw, w2_hi[:, :, :].bitcast(FP32), ALU.subtract)\
                .then_inc(mlp_lo, 1)
            dve.wait_ge(bias_mm, 2)
            nc.vector.tensor_tensor(mlp_bias[:, :], bias_ps[:, 3 * KT:3 * KT + FT], b1_cols[:, :], ALU.add)\
                .then_inc(bias_done, 1)

            def pair(i, first, ahead):
                wait(dve, mask_done, i + 1)
                scores(2 * i, 0)
                if not first:
                    weights_out(2 * i - 1)
                reciprocals(2 * i, 0)
                if ahead >= 2:
                    pair_stats(i + 2)
                if not first:
                    heads_out(2 * i - 1)
                reciprocals(2 * i, 1)
                if ahead >= 1:
                    lower_half(i + 1)
                if not first:
                    residual(i - 1, 2 * i - 1)
                scores(2 * i + 1, 1)
                if ahead >= 1:
                    masks(i + 1)
                weights_out(2 * i)
                reciprocals(2 * i + 1, 0)
                if ahead >= 2:
                    pair_norm(i + 2)
                heads_out(2 * i)
                reciprocals(2 * i + 1, 1)
                if ahead >= 1:
                    key_blocks(i + 1)
                residual(i, 2 * i)

            pair(0, True, 2)
            with nc.vector.Fori(1, PAIRS - 2) as i:
                pair(i, False, 2)
            pair(PAIRS - 2, False, 1)
            pair(PAIRS - 1, False, 0)
            weights_out(G - 1)
            heads_out(G - 1)
            residual(PAIRS - 1, G - 1)

            def block_stats(t):
                for j in range(BG):
                    nc.vector.bn_stats(stats2[:, j, :], xs[:, BG * t + j, :]).then_inc(stats2_done, 1)
                for j in range(BG):
                    wait(dve, stats2_done, BG * t + j + 1)
                    apart(dve)
                    nc.vector.bn_aggr(mv2[:, j, :], stats2[:, j, :]).then_inc(mv2_done, 1)
                wait(dve, mv2_done, BG * t + BG)
                nc.vector.tensor_scalar(var_eps2[:, :], mv2[:, :, 1], EPS, None, ALU.add)\
                    .then_inc(var2_done, 1)

            def block_norm(t):
                wait(dve, rstd2_done, t + 1)
                wait(dve, t2_mm, KT * t)
                for j in range(BG):
                    last = nc.vector.tensor_scalar(nx2[:, j, :], xs[:, BG * t + j, :], mv2[:, j, 0:1],
                                                   rstd2[:, j:j + 1], ALU.subtract, ALU.mult)
                last.then_inc(nx2_done, 1)

            def lower_half2(t):
                for k in range(KT):
                    wait(dve, n2_hi_done, KT * t + k + 1)
                    nc.vector.tensor_tensor(n2_lo[:, k, :], t2_ps[k][:, :], n2_hi[:, k, :].bitcast(FP32),
                                            ALU.subtract).then_inc(n2_lo_done, 1)

            def halves(t, f):
                u = f % 2
                wait(dve, gelu_done, FT * t + f + 1)
                wait(dve, w2_mm, FT * t + f - 1)
                nc.vector.tensor_copy(h_hi[:, u, :], h_sb[:, u, :]).then_inc(h_hi_done, 1)
                wait(dve, h_hi_done, FT * t + f + 1)
                nc.vector.tensor_tensor(h_lo[:, u, :], h_sb[:, u, :], h_hi[:, u, :].bitcast(FP32),
                                        ALU.subtract).then_inc(h_lo_done, 1)

            def outputs(t):
                wait(dve, w2_mm, FT * t + FT)
                wait(dve, xb2_done, t + 1)
                for j in range(BG):
                    nc.vector.tensor_tensor(xs[:, BG * t + j, :], y_ps[j], xs[:, BG * t + j, :], ALU.add)\
                        .then_inc(y_out, 1)

            def mlp_block(t, first, last):
                if not first:
                    outputs(t - 1)
                for f in range(FT):
                    halves(t, f)
                    if f == 0 and not last:
                        block_stats(t + 1)
                    if f == 2 and not last:
                        block_norm(t + 1)
                if not last:
                    lower_half2(t + 1)

            dve.wait_ge(mlp_lo, KT + 1)
            dve.wait_ge(x1_done, G)
            block_stats(0)
            block_norm(0)
            lower_half2(0)
            mlp_block(0, True, False)
            with nc.vector.Fori(1, BLOCKS - 1) as t:
                mlp_block(t, False, False)
            mlp_block(BLOCKS - 1, False, True)
            outputs(BLOCKS - 1)

        @block.tensor
        def _(pe):
            def split_product(dst, hi, lo, rhs_hi, rhs_lo, ks):
                terms = [(a, b, k) for a, b in ((hi, rhs_hi), (hi, rhs_lo), (lo, rhs_hi)) for k in ks]
                for n, (a, b, k) in enumerate(terms):
                    mm = nc.tensor.matmul(dst, a(k), b(k), start=(n == 0), stop=(n == len(terms) - 1))
                return mm

            def transposed(i):
                wait(pe, nx_done, i + 1)
                wait(pe, q_out, KT * i)
                for j in range(2):
                    for k in range(KT):
                        mm = nc.tensor.transpose(tq_ps[:, k, j * S:(j + 1) * S],
                                                 nx[:, j, k * P:(k + 1) * P], ident[:, :])
                mm.then_inc(t_done, 1)

            def project(n, dst):
                for m in range(KT):
                    cols = slice(m * P, (m + 1) * P)
                    mm = split_product(dst[:, m, :], lambda k: wqkv_hi[:, n, k, cols],
                                       lambda k: wqkv_lo[:, n, k, cols],
                                       lambda k: nt_hi[:, k, :], lambda k: nt_lo[:, k, :], range(KT))
                return mm

            def keys(i):
                wait(pe, hi_done, i + 1)
                wait(pe, lo_done, i + 1)
                wait(pe, k_act, HPT * i)
                wait(pe, k_dve, HPT * i)
                project(1, k_ps).then_inc(k_mm, 1)

            def queries(i):
                project(0, tq_ps).then_inc(q_mm, 1)

            def values(i):
                wait(pe, v_out, i)
                for j in range(2):
                    toks = slice(j * S, (j + 1) * S)
                    mm = split_product(v_ps[:, j, :], lambda k: nt_hi[:, k, toks],
                                       lambda k: nt_lo[:, k, toks], lambda k: wqkv_hi[:, 2, k, :],
                                       lambda k: wqkv_lo[:, 2, k, :], range(KT))
                mm.then_inc(v_mm, 1)

            def scores(g, j):
                wait(pe, z_done, HEADS * g)
                for k in range(KT):
                    nc.tensor.matmul(s_ps[k], qT[:, k, j * S:(j + 1) * S],
                                     kz[:, k, :, j * S:(j + 1) * S], start=True, stop=True)\
                        .then_inc(s_mm, 1)

            def weights_transposed(g):
                for k in range(KT):
                    wait(pe, p_done, 2 * g + k + 1)
                    if k == 0:
                        wait(pe, pt_act, g)
                    else:
                        wait(pe, pt_dve, g)
                    for h in range(HPT):
                        mm = nc.tensor.transpose(pt_ps[k][:, h, :], p_sb[:, HPT * k + h, :], ident[:, :])
                    mm.then_inc(pt_mm, 1)

            def weighted_values(i, g, j):
                wait(pe, v_out, i + 1)
                wait(pe, pt_act, g + 1)
                wait(pe, pt_dve, g + 1)
                wait(pe, x1_done, g)
                for h in range(HEADS):
                    mm = nc.tensor.matmul(o_ps[D * (h % HPT):D * (h % HPT) + D, h // HPT, :],
                                          v_sb[:, j, D * h:D * h + D], pT[:, h, :], start=True, stop=True)
                mm.then_inc(pv_mm, 1)

            def out_projection(g):
                wait(pe, o_out, g + 1)
                for k in range(KT):
                    mm = nc.tensor.matmul(wo_ps, oT[:, k, :], wo_sb[:, k, :], start=(k == 0),
                                          stop=(k == KT - 1))
                mm.then_inc(wo_mm, 1)

            def pair(i, first, last):
                wait(pe, k_act, HPT * i + HPT)
                wait(pe, k_dve, HPT * i + HPT)
                wait(pe, q_out, KT * i + KT)
                scores(2 * i, 0)
                if not first:
                    weights_transposed(2 * i - 1)
                values(i)
                if not first:
                    weighted_values(i - 1, 2 * i - 1, 1)
                if not last:
                    transposed(i + 1)
                if not first:
                    out_projection(2 * i - 1)
                scores(2 * i + 1, 1)
                weights_transposed(2 * i)
                if not last:
                    keys(i + 1)
                weighted_values(i, 2 * i, 0)
                if not last:
                    queries(i + 1)
                out_projection(2 * i)

            pe.wait_ge(consts, 2)
            transposed(0)
            pe.wait_ge(qkv_in, 48)
            pe.wait_ge(small_in, 128)
            bias_ps = bank[7]
            for n in range(3):
                for m in range(KT):
                    for k in range(KT):
                        mm = nc.tensor.matmul(bias_ps[:, n * KT + m:n * KT + m + 1],
                                              qkv_raw[:, n, k, m * P:(m + 1) * P], ln_cols[:, 1, k:k + 1],
                                              start=(k == 0), stop=(k == KT - 1))
            mm.then_inc(bias_mm, 1)
            pe.wait_ge(w_lo, 3 * KT)
            keys(0)
            queries(0)
            pe.wait_ge(wo_in, 16)
            pe.wait_ge(bv_done, 1)
            for k in range(KT):
                mm = nc.tensor.matmul(wo_ps, bv_wide[:, k, :], wo_sb[:, k, :], start=(k == 0), stop=(k == KT - 1))
            mm.then_inc(bo_mm, 1)
            pe.wait_ge(mlp_in, 32)
            pe.wait_ge(bo_done, 1)
            for f in range(FT):
                for k in range(KT):
                    mm = nc.tensor.matmul(bias_ps[:, 3 * KT + f:3 * KT + f + 1], w1_raw[:, k, f * P:(f + 1) * P],
                                          ln_cols[:, 3, k:k + 1], start=(k == 0), stop=(k == KT - 1))
            mm.then_inc(bias_mm, 1)
            pe.wait_ge(bias_done, 2)
            pair(0, True, False)
            with nc.tensor.Fori(1, PAIRS - 1) as i:
                pair(i, False, False)
            pair(PAIRS - 1, False, True)
            weights_transposed(G - 1)
            weighted_values(PAIRS - 1, G - 1, 1)
            out_projection(G - 1)

            def transposed2(t):
                wait(pe, nx2_done, t + 1)
                wait(pe, n2_lo_done, KT * t)
                for k in range(KT):
                    for j in range(BG):
                        mm = nc.tensor.transpose(t2_ps[k][:, j * S:(j + 1) * S],
                                                 nx2[:, j, k * P:(k + 1) * P], ident[:, :])
                    mm.then_inc(t2_mm, 1)

            def up(t, f):
                wait(pe, gelu_done, FT * t + f - 1)
                cols = slice(f * P, (f + 1) * P)
                split_product(h_ps[f % 2][:, :], lambda k: w1_hi[:, k, cols], lambda k: w1_lo[:, k, cols],
                              lambda k: n2_hi[:, k, :], lambda k: n2_lo[:, k, :], range(KT)).then_inc(w1_mm, 1)

            def down(t, f):
                wait(pe, h_lo_done, FT * t + f + 1)
                if f == 0:
                    wait(pe, y_out, BG * t)
                u = f % 2
                for j in range(BG):
                    toks = slice(j * S, (j + 1) * S)
                    for n, (a, b) in enumerate(((h_hi, w2_hi), (h_hi, w2_lo), (h_lo, w2_hi))):
                        mm = nc.tensor.matmul(y_ps[j], a[:, u, toks], b[:, f, :],
                                              start=(f == 0 and n == 0), stop=(f == FT - 1 and n == 2))
                mm.then_inc(w2_mm, 1)

            def mlp_block(t, last):
                wait(pe, n2_lo_done, KT * t + KT)
                for f in range(FT):
                    up(t, f)
                    if f >= 1:
                        down(t, f - 1)
                    if f == FT - 2 and not last:
                        transposed2(t + 1)
                down(t, FT - 1)

            pe.wait_ge(x1_done, G)
            transposed2(0)
            mlp_block(0, False)
            with nc.tensor.Fori(1, BLOCKS - 1) as t:
                mlp_block(t, False)
            mlp_block(BLOCKS - 1, True)


def kernel(**inputs):
    import numpy as np
    import concourse.bacc as bacc
    from concourse import mybir
    from concourse.bass_utils import run_bass_kernel_spmd

    def columns(v):
        return np.ascontiguousarray(np.asarray(v).reshape(-1, 128).T)

    def plain(v):
        return np.ascontiguousarray(np.asarray(v))

    pre = "L0_gnn_"
    arrays = {
        "x": plain(inputs["x"]),
        "adj": np.ascontiguousarray(np.asarray(inputs["adj"]).transpose(1, 0, 2)),
    }
    for n in ("ln1_g", "ln1_b", "ln2_g", "ln2_b"):
        arrays[n] = columns(inputs[pre + n])
    for n in ("q", "k", "v", "o"):
        arrays["w" + n] = plain(inputs[pre + "W" + n])
        arrays["b" + n] = (plain if n == "o" else columns)(inputs[pre + "b" + n])
    for n in ("1", "2"):
        arrays["w" + n] = plain(inputs[pre + "W" + n])
        arrays["b" + n] = (plain if n == "2" else columns)(inputs[pre + "b" + n])

    nc = bacc.Bacc("TRN2", target_bir_lowering=False, num_devices=1)
    aps = {n: nc.dram_tensor(f"in_{n}", a.shape, mybir.dt.from_np(a.dtype), kind="ExternalInput").ap()
           for n, a in arrays.items()}
    out = nc.dram_tensor("out", arrays["x"].shape, mybir.dt.float32, kind="ExternalOutput").ap()
    build_gnn_layer(nc, out=out, **aps)
    r = run_bass_kernel_spmd(nc, [{f"in_{n}": a for n, a in arrays.items()}], core_ids=[0])
    return r.results[0]["out"]
```

```python
import concourse.bass as bass
from concourse import mybir
from contextlib import ExitStack

FP32 = mybir.dt.float32
F32R = mybir.dt.float32r
U8 = mybir.dt.uint8
ALU = mybir.AluOpType
ACT = mybir.ActivationFunctionType

P = 128
EPS = 1e-5
MASKED = 1e30


def build_gnn_layer(nc, x, adj, ln1_g, ln1_b, ln2_g, ln2_b, wq, bq, wk, bk, wv, bv, wo, bo,
                    w1, b1, w2, b2, out):
    G, S, H = x.shape
    HEADS = 8
    D = H // HEADS
    FF = w1.shape[1]
    KT = H // P
    HPT = P // D
    FT = FF // P
    PAIRS = G // 2
    T2 = 2 * S
    BG = 4
    TB = BG * S
    BLOCKS = G // BG
    SCALE = float(D) ** -0.5
    assert S == P and H == 2 * P and HPT == 4 and FT == 8

    ctx = ExitStack()
    with ctx:
        def sb(name, shape, dt=FP32):
            return ctx.enter_context(nc.sbuf_tensor(name, shape, dt))

        def sem(name):
            return ctx.enter_context(nc.semaphore(name))

        xs = sb("xs", [P, G, H])
        adj_u8 = sb("adj_u8", [P, 2, S], U8)
        first_f32 = sb("first_f32", [P, 3 * KT * H])
        qkv_raw = first_f32[:, :].rearrange("p (n k c) -> p n k c", n=3, k=KT)
        wqkv_hi = sb("wqkv_hi", [P, 3, KT, H], F32R)
        wqkv_lo = sb("wqkv_lo", [P, 3, KT, H], F32R)
        wo_sb = sb("wo_sb", [P, KT, H])
        w1_hi = sb("w1_hi", [P, KT, FF], F32R)
        w1_lo = sb("w1_lo", [P, KT, FF], F32R)
        w2_hi = sb("w2_hi", [P, FT, H], F32R)
        w2_lo = sb("w2_lo", [P, FT, H], F32R)
        GW = FF * KT // H
        LATE = (G - 2 * GW) // 2
        w1_raw = xs[:, G - 2 * GW:G - GW, :].rearrange("p (k g) c -> p k (g c)", k=KT)
        w2_raw = xs[:, G - GW:G, :]
        ln_cols = sb("ln_cols", [P, 4, KT])
        bias_cols = sb("bias_cols", [P, 3, KT])
        b1_cols = sb("b1_cols", [P, FT])
        qkv_bias = sb("qkv_bias", [P, 3, KT])
        mlp_bias = sb("mlp_bias", [P, FT])
        bv_wide = sb("bv_wide", [P, KT, P])
        bo_rows = sb("bo_rows", [P, H])
        b2_rows = sb("b2_rows", [P, H])
        out_bias = sb("out_bias", [P, H])
        ident = sb("ident", [P, P])
        minus_half = sb("minus_half", [P, BG])

        stats = sb("stats", [P, 2, 6])
        mv = sb("mv", [P, 2, 2])
        var_eps = sb("var_eps", [P, 2])
        rstd = sb("rstd", [P, 2])
        nx = sb("nx", [P, 2, H])
        nt_all = sb("nt_all", [P, 2 * 2 * KT * T2], F32R)
        nt = [nt_all[:, par * 2 * KT * T2:(par + 1) * 2 * KT * T2]
              .rearrange("p (u k t) -> p u k t", u=2, k=KT) for par in range(2)]
        nt_hi = [nt[par][:, 0, :, :] for par in range(2)]
        nt_lo = [nt[par][:, 1, :, :] for par in range(2)]
        q_hi = sb("q_hi", [P, KT, T2], F32R)
        q_lo = sb("q_lo", [P, KT, T2], F32R)
        k_halves = sb("k_halves", [P, 2, KT, T2], F32R)
        kz_all = sb("kz_all", [P, 2 * KT * HPT * T2], F32R)
        kz = kz_all[:, :].rearrange("p (u k j t) -> p u k j t", u=2, k=KT, j=HPT)
        v_sb = sb("v_sb", [P, 2, H])
        mask_add = sb("mask_add", [P, 2, S])
        z_all = sb("z_all", [P, HEADS * S])
        z_neg = z_all[:, :].rearrange("p (h k) -> p h k", h=HEADS)
        min_z = sb("min_z", [P, HEADS])
        e_sb = sb("e_sb", [P, HEADS, S])
        sums = sb("sums", [P, HEADS])
        rinv = sb("rinv", [P, HEADS])
        p_sb = sb("p_sb", [P, HEADS, S])
        pT = sb("pT", [P, HEADS, S])
        oT = sb("oT", [P, KT, S])

        stats2 = sb("stats2", [P, BG, 6])
        mv2 = sb("mv2", [P, BG, 2])
        var_eps2 = sb("var_eps2", [P, BG])
        rstd2 = sb("rstd2", [P, BG])
        nx2 = first_f32[:, 0:BG * H].rearrange("p (g c) -> p g c", g=BG)
        h_sb = z_all[:, :].rearrange("p (u t) -> p u t", u=2)
        n2_even = nt_all[:, :].rearrange("p (u k t) -> p u k t", u=2, k=KT)
        part = 2 * KT * TB
        n2_odd = kz_all[:, 0:part].rearrange("p (u k t) -> p u k t", u=2, k=KT)
        h_hi = kz_all[:, part:part + 2 * TB].rearrange("p (u t) -> p u t", u=2)
        h_lo = kz_all[:, part + 2 * TB:part + 4 * TB].rearrange("p (u t) -> p u t", u=2)
        n2_hi = [n2_even[:, 0, :, :], n2_odd[:, 0, :, :]]
        n2_lo = [n2_even[:, 1, :, :], n2_odd[:, 1, :, :]]

        bank = [ctx.enter_context(nc.psum_tensor(f"bank{n}", [P, 512], FP32)) for n in range(8)]
        t_ps = bank[6][:, :].rearrange("p (k t) -> p k t", k=KT)
        k_ps = [bank[1][:, 0:T2], bank[0][:, 0:T2]]
        q_ps = [bank[0][:, 0:T2], bank[1][:, 0:T2]]
        v_ps = bank[2][:, :].rearrange("p (g c) -> p g c", g=2)
        s_ps = [bank[3 + k][:, :].rearrange("p (h k) -> p h k", h=HPT) for k in range(KT)]
        pt_ps = [bank[5 + k][:, :].rearrange("p (h q) -> p h q", h=HPT) for k in range(KT)]
        o_ps = bank[7][:, 0:H].rearrange("p (k q) -> p k q", k=KT)
        wo_ps = bank[7][:, H:2 * H]
        t2_ps = [bank[k] for k in range(KT)]
        h_ps = [bank[2], bank[3]]
        y_ps = [bank[4 + j][:, 0:H] for j in range(BG)]

        wait_taken = sem("wait_taken")
        sp_wait_taken = sem("sp_wait_taken")
        pool_wait_taken = sem("pool_wait_taken")
        x_in = sem("x_in")
        adj_in = sem("adj_in")
        qkv_in = sem("qkv_in")
        small_in = sem("small_in")
        rows_in = sem("rows_in")
        wo_in = sem("wo_in")
        mlp_in = sem("mlp_in")
        out_done = sem("out_done")
        id_zero = sem("id_zero")
        consts = sem("consts")
        kz_zero = sem("kz_zero")
        w_hi = sem("w_hi")
        w_lo = sem("w_lo")
        mlp_hi = sem("mlp_hi")
        mlp_lo = sem("mlp_lo")
        bias_mm = sem("bias_mm")
        bias_done = sem("bias_done")
        bv_done = sem("bv_done")
        bo_mm = sem("bo_mm")
        bo_done = sem("bo_done")

        stats_done = sem("stats_done")
        mv_done = sem("mv_done")
        var_done = sem("var_done")
        rstd_done = sem("rstd_done")
        nx_done = sem("nx_done")
        mask_done = sem("mask_done")
        xb_done = sem("xb_done")
        t_done = sem("t_done")
        hi_done = sem("hi_done")
        lo_done = sem("lo_done")
        k_mm = sem("k_mm")
        q0_mm = sem("q0_mm")
        q_mm = sem("q_mm")
        v_mm = sem("v_mm")
        k_hi_done = sem("k_hi_done")
        k_lo_done = sem("k_lo_done")
        kz_in = sem("kz_in")
        q_hi_done = sem("q_hi_done")
        q_lo_done = sem("q_lo_done")
        v_out = sem("v_out")
        s_mm = sem("s_mm")
        z_done = sem("z_done")
        e_done = sem("e_done")
        rinv_done = sem("rinv_done")
        p_done = sem("p_done")
        pt_mm = sem("pt_mm")
        pt_first = sem("pt_first")
        pt_second = sem("pt_second")
        pv_mm = sem("pv_mm")
        o_out = sem("o_out")
        wo_mm = sem("wo_mm")
        x1_done = sem("x1_done")

        stats2_done = sem("stats2_done")
        mv2_done = sem("mv2_done")
        var2_done = sem("var2_done")
        rstd2_done = sem("rstd2_done")
        nx2_done = sem("nx2_done")
        xb2_done = sem("xb2_done")
        t2_mm = sem("t2_mm")
        n2_hi_done = sem("n2_hi_done")
        n2_lo_done = sem("n2_lo_done")
        w1_mm = sem("w1_mm")
        gelu_done = sem("gelu_done")
        h_hi_done = sem("h_hi_done")
        h_lo_done = sem("h_lo_done")
        w2_mm = sem("w2_mm")
        y_out = sem("y_out")

        def wait(eng, s, value):
            if not isinstance(value, int) or value > 0:
                eng.wait_ge(s, value)

        def apart(dve):
            dve.sem_inc(wait_taken, 1)

        block = ctx.enter_context(nc.Block())

        @block.sync
        def _(sp):
            x_pairs = x.rearrange("g p c -> p g c")
            out_blocks = out.rearrange("g p c -> p g c")

            def load_pair(i):
                wait(sp, x_in, 16 * i)
                sp.dma_start(xs[:, bass.ts(i, 2), :], x_pairs[:, bass.ts(i, 2), :]).then_inc(x_in, 16)

            def load_edges(i):
                wait(sp, mask_done, i)
                sp.dma_start(adj_u8[:, :, :], adj[:, bass.ts(i, 2), :]).then_inc(adj_in, 16)

            def spread_keys(i):
                wait(sp, k_lo_done, KT * i + KT)
                sp.sem_inc(sp_wait_taken, 1)
                wait(sp, s_mm, 4 * i)
                for j in range(HPT):
                    q = slice(D * j, D * j + D)
                    sp.dma_start(kz[q, :, :, j, :].rearrange("p u k t -> p (u k) t").bitcast(FP32),
                                 k_halves[q, :, :, :].rearrange("p u k t -> p (u k) t").bitcast(FP32)).then_inc(kz_in, 16)

            load_pair(0)
            load_edges(0)
            load_pair(1)
            sp.dma_start(wo_sb[:, :, :], wo.rearrange("(k p) n -> p k n", p=P)).then_inc(wo_in, 16)
            sp.dma_start(w1_raw, w1.rearrange("(k p) n -> p k n", p=P)).then_inc(mlp_in, 16)
            sp.dma_start(w2_raw, w2.rearrange("(f p) n -> p f n", p=P)).then_inc(mlp_in, 16)
            load_pair(2)
            sp.wait_ge(kz_zero, 1)
            load_edges(1)
            spread_keys(0)
            with nc.sync.Fori(3, LATE) as i:
                spread_keys(i - 2)
                load_pair(i)
                load_edges(i - 1)
            sp.wait_ge(mlp_lo, KT + 1)
            sp.wait_ge(bias_mm, 2)
            with nc.sync.Fori(LATE, PAIRS) as i:
                spread_keys(i - 2)
                load_pair(i)
                load_edges(i - 1)
            spread_keys(PAIRS - 2)
            load_edges(PAIRS - 1)
            spread_keys(PAIRS - 1)
            with nc.sync.Fori(0, BLOCKS) as t:
                sp.wait_ge(y_out, BG * t + BG)
                sp.dma_start(out_blocks[:, bass.ts(t, BG), :], xs[:, bass.ts(t, BG), :])\
                    .then_inc(out_done, 16)
            sp.wait_ge(out_done, 16 * BLOCKS)

        @block.gpsimd
        def _(pool):
            nc.gpsimd.memset(ident[:, :], 0.0).then_inc(id_zero, 1)
            pool.wait_ge(id_zero, 1)
            nc.gpsimd.affine_select(out=ident[:, :], in_=ident[:, :], compare_op=ALU.not_equal,
                                    fill=1.0, base=0, pattern=[[-1, P]], channel_multiplier=1)\
                .then_inc(consts, 1)
            nc.gpsimd.memset(minus_half[:, :], -0.5).then_inc(consts, 1)
            pool.wait_ge(consts, 2)
            for n, row in enumerate((bo, b2)):
                dst = (bo_rows, b2_rows)[n]
                nc.gpsimd.dma_start(dst[:, :], row.partition_broadcast(P)).then_inc(rows_in, 16)

            def inv_std(i):
                wait(pool, var_done, i + 1)
                wait(pool, nx_done, i)
                nc.gpsimd.tensor_tensor(rstd[:, :], var_eps[:, :], minus_half[:, 0:2], ALU.pow)\
                    .then_inc(rstd_done, 1)

            def normalise(g, k):
                wait(pool, rinv_done, 2 * g + k + 1)
                wait(pool, pt_mm, 2 * g - 1 + k)
                hs = slice(HPT * k, HPT * k + HPT)
                nc.gpsimd.tensor_tensor(p_sb[:, hs, :], e_sb[:, hs, :],
                                        rinv[:, hs].unsqueeze(2).to_broadcast([P, HPT, S]),
                                        ALU.mult).then_inc(p_done, 1)

            def add_out_bias(i):
                wait(pool, nx_done, i + 1)
                nc.gpsimd.tensor_tensor(xs[:, bass.ts(i, 2), :], xs[:, bass.ts(i, 2), :],
                                        out_bias[:, :].unsqueeze(1).to_broadcast([P, 2, H]),
                                        ALU.add).then_inc(xb_done, 1)

            def inv_std2(t):
                wait(pool, var2_done, t + 1)
                nc.gpsimd.tensor_tensor(rstd2[:, :], var_eps2[:, :], minus_half[:, :], ALU.pow)\
                    .then_inc(rstd2_done, 1)

            def masks(i):
                wait(pool, adj_in, 16 * i + 16)
                wait(pool, z_done, 2 * HEADS * i)
                pool.sem_inc(pool_wait_taken, 1)
                nc.gpsimd.tensor_scalar(mask_add[:, :, :], adj_u8[:, :, :], MASKED, -MASKED, ALU.mult,
                                        ALU.add).then_inc(mask_done, 1)

            def pair(i, ahead):
                normalise(2 * i, 0)
                normalise(2 * i, 1)
                if ahead >= 2:
                    inv_std(i + 2)
                if ahead == 0:
                    inv_std2(0)
                if ahead >= 1:
                    masks(i + 1)
                normalise(2 * i + 1, 0)
                normalise(2 * i + 1, 1)
                if ahead >= 1:
                    add_out_bias(i + 1)

            inv_std(0)
            masks(0)
            inv_std(1)
            pool.wait_ge(bo_done, 1)
            add_out_bias(0)
            pair(0, 2)
            with nc.gpsimd.Fori(1, PAIRS - 2) as i:
                pair(i, 2)
            pair(PAIRS - 2, 1)
            pair(PAIRS - 1, 0)

            def add_mlp_bias(t):
                wait(pool, nx2_done, t + 1)
                nc.gpsimd.tensor_tensor(xs[:, bass.ts(t, BG), :], xs[:, bass.ts(t, BG), :],
                                        b2_rows[:, :].unsqueeze(1).to_broadcast([P, BG, H]),
                                        ALU.add).then_inc(xb2_done, 1)

            add_mlp_bias(0)
            with nc.gpsimd.Fori(1, BLOCKS) as t:
                inv_std2(t)
                add_mlp_bias(t)

        @block.scalar
        def _(act):
            for n, w in enumerate((wq, wk, wv)):
                act.dma_start(qkv_raw[:, n, :, :], w.rearrange("(k p) n -> p k n", p=P))\
                    .then_inc(qkv_in, 16)
            for n, v in enumerate((ln1_g, ln1_b, ln2_g, ln2_b)):
                act.dma_start(ln_cols[:, n, :], v).then_inc(small_in, 16)
            for n, v in enumerate((bq, bk, bv)):
                act.dma_start(bias_cols[:, n, :], v).then_inc(small_in, 16)
            act.dma_start(b1_cols[:, :], b1).then_inc(small_in, 16)

            act.wait_ge(qkv_in, 48)
            act.wait_ge(small_in, 128)
            for n in range(3):
                for k in range(KT):
                    nc.scalar.activation(wqkv_hi[:, n, k, :], qkv_raw[:, n, k, :], ACT.Copy,
                                         scale=ln_cols[:, 0, k:k + 1]).then_inc(w_hi, 1)

            def upper_half(i, par):
                wait(act, t_done, i + 1)
                wait(act, q_mm, i - 1)
                nc.scalar.activation(nt_hi[par], t_ps, ACT.Copy).then_inc(hi_done, 1)

            def keys_hi(i):
                wait(act, kz_in, 16 * HPT * i)
                for k in range(KT):
                    wait(act, k_mm, KT * i + k + 1)
                    nc.scalar.activation(k_halves[:, 0, k, :], k_ps[k], ACT.Identity,
                                         bias=qkv_bias[:, 1, k:k + 1]).then_inc(k_hi_done, 1)

            def queries_hi(i, k):
                wait(act, q0_mm if k == 0 else q_mm, i + 1)
                wait(act, s_mm, 4 * i)
                nc.scalar.activation(q_hi[:, k, :], q_ps[k], ACT.Identity,
                                     bias=qkv_bias[:, 0, k:k + 1]).then_inc(q_hi_done, 1)

            def values(i):
                wait(act, v_mm, 2 * i + 2)
                wait(act, pv_mm, 2 * i)
                nc.scalar.activation(v_sb[:, :, :], v_ps, ACT.Copy).then_inc(v_out, 1)

            def exps(g, heads):
                for h in heads:
                    wait(act, z_done, HEADS * g + h + 1)
                    if h % HPT == 0:
                        wait(act, p_done, 2 * g - 1 + h // HPT)
                    nc.scalar.activation(e_sb[:, h, :], z_neg[:, h, :], ACT.Exp,
                                         bias=min_z[:, h:h + 1], scale=-1.0,
                                         accum_out=sums[:, h:h + 1]).then_inc(e_done, 1)

            def weights_out(g):
                wait(act, pt_mm, 2 * g + 1)
                wait(act, pv_mm, g)
                nc.scalar.activation(pT[:, 0:HPT, :], pt_ps[0], ACT.Copy).then_inc(pt_first, 1)

            def pair(i, par, first, ahead):
                exps(2 * i, range(0, 3))
                if not first:
                    weights_out(2 * i - 1)
                exps(2 * i, range(3, 5))
                if ahead >= 1:
                    keys_hi(i + 1)
                exps(2 * i, range(5, 6))
                values(i)
                exps(2 * i, range(6, HEADS))
                exps(2 * i + 1, range(0, 4))
                weights_out(2 * i)
                exps(2 * i + 1, range(4, 6))
                if ahead >= 1:
                    queries_hi(i + 1, 0)
                exps(2 * i + 1, range(6, HEADS))
                if ahead >= 2:
                    upper_half(i + 2, par)
                if ahead >= 1:
                    queries_hi(i + 1, 1)

            def upper_half2(t, par):
                for k in range(KT):
                    wait(act, t2_mm, KT * t + k + 1)
                    wait(act, w1_mm, FT * (t - 1))
                    nc.scalar.activation(n2_hi[par][:, k, :], t2_ps[k][:, :], ACT.Copy)\
                        .then_inc(n2_hi_done, 1)

            upper_half(0, 0)
            act.wait_ge(bias_done, 1)
            keys_hi(0)
            queries_hi(0, 0)
            queries_hi(0, 1)
            act.wait_ge(mlp_in, 32)
            for k in range(KT):
                nc.scalar.activation(w1_hi[:, k, :], w1_raw[:, k, :], ACT.Copy,
                                     scale=ln_cols[:, 2, k:k + 1]).then_inc(mlp_hi, 1)
            nc.scalar.activation(w2_hi[:, :, :], w2_raw, ACT.Copy).then_inc(mlp_hi, 1)
            upper_half(1, 1)
            pair(0, 0, True, 2)
            with nc.scalar.Fori(0, (PAIRS - 4) // 2) as u:
                pair(2 * u + 1, 1, False, 2)
                pair(2 * u + 2, 0, False, 2)
            pair(PAIRS - 3, 1, False, 2)
            pair(PAIRS - 2, 0, False, 1)
            pair(PAIRS - 1, 1, False, 0)
            upper_half2(0, 0)
            weights_out(G - 1)

            def gelu(t, f):
                wait(act, w1_mm, FT * t + f + 1)
                wait(act, h_lo_done, FT * t + f - 1)
                nc.scalar.activation(h_sb[:, f % 2, :], h_ps[f % 2][:, :], ACT.Gelu,
                                     bias=mlp_bias[:, f:f + 1]).then_inc(gelu_done, 1)

            def mlp_block(t, par, last):
                for f in range(FT):
                    gelu(t, f)
                    if f == 4 and not last:
                        upper_half2(t + 1, 1 - par)

            mlp_block(0, 0, False)
            with nc.scalar.Fori(0, (BLOCKS - 2) // 2) as u:
                mlp_block(2 * u + 1, 1, False)
                mlp_block(2 * u + 2, 0, False)
            mlp_block(BLOCKS - 1, 1, True)

        @block.vector
        def _(dve):
            nc.vector.memset(kz_all[:, :].bitcast(FP32), 0.0).then_inc(kz_zero, 1)

            def pair_stats(i):
                wait(dve, x_in, 16 * i + 16)
                for j in range(2):
                    nc.vector.bn_stats(stats[:, j, :], xs[:, 2 * i + j, :]).then_inc(stats_done, 1)

            def pair_variances(i):
                for j in range(2):
                    wait(dve, stats_done, 2 * i + j + 1)
                    apart(dve)
                    nc.vector.bn_aggr(mv[:, j, :], stats[:, j, :]).then_inc(mv_done, 1)
                wait(dve, mv_done, 2 * i + 2)
                wait(dve, rstd_done, i)
                nc.vector.tensor_scalar(var_eps[:, :], mv[:, :, 1], EPS, None, ALU.add)\
                    .then_inc(var_done, 1)

            def pair_norm(i):
                wait(dve, rstd_done, i + 1)
                wait(dve, t_done, i)
                for j in range(2):
                    last = nc.vector.tensor_scalar(nx[:, j, :], xs[:, 2 * i + j, :], mv[:, j, 0:1],
                                                   rstd[:, j:j + 1], ALU.subtract, ALU.mult)
                last.then_inc(nx_done, 1)

            def scores(g, j, k):
                wait(dve, e_done, HEADS * (g - 1) + HPT * (k + 1))
                wait(dve, s_mm, 2 * g + k + 1)
                apart(dve)
                for h in range(HPT * k, HPT * k + HPT):
                    nc.vector.tensor_tensor_reduce(
                        out=z_neg[:, h, :], in0=s_ps[h // HPT][:, h % HPT, :], in1=mask_add[:, j, :],
                        scale=-SCALE, scalar=3e38, op0=ALU.add, op1=ALU.min,
                        accum_out=min_z[:, h:h + 1]).then_inc(z_done, 1)

            def reciprocals(g, k):
                wait(dve, e_done, HEADS * g + HPT * (k + 1))
                hs = slice(HPT * k, HPT * k + HPT)
                nc.vector.reciprocal(rinv[:, hs], sums[:, hs]).then_inc(rinv_done, 1)

            def weights_out(g):
                wait(dve, pt_mm, 2 * g + 2)
                wait(dve, pv_mm, g)
                nc.vector.tensor_copy(pT[:, HPT:HEADS, :], pt_ps[1]).then_inc(pt_second, 1)

            def heads_out(g):
                wait(dve, pv_mm, g + 1)
                wait(dve, wo_mm, g)
                nc.vector.tensor_copy(oT[:, :, :], o_ps).then_inc(o_out, 1)

            def residual(i, g):
                wait(dve, wo_mm, g + 1)
                wait(dve, xb_done, i + 1)
                nc.vector.tensor_tensor(xs[:, g, :], wo_ps, xs[:, g, :], ALU.add).then_inc(x1_done, 1)

            def lower_half(i, par):
                wait(dve, hi_done, i + 1)
                wait(dve, q_mm, i - 1)
                nc.vector.tensor_tensor(nt_lo[par], t_ps, nt_hi[par].bitcast(FP32), ALU.subtract)\
                    .then_inc(lo_done, 1)

            def keys_lo(i):
                wait(dve, kz_in, 16 * HPT * i)
                for k in range(KT):
                    wait(dve, k_hi_done, KT * i + k + 1)
                    nc.vector.scalar_tensor_tensor(
                        out=k_halves[:, 1, k, :], in0=k_ps[k], scalar=qkv_bias[:, 1, k:k + 1],
                        in1=k_halves[:, 0, k, :].bitcast(FP32), op0=ALU.add, op1=ALU.subtract)\
                        .then_inc(k_lo_done, 1)

            def queries_lo(i, k):
                wait(dve, q_hi_done, KT * i + k + 1)
                wait(dve, s_mm, 4 * i)
                nc.vector.scalar_tensor_tensor(
                    out=q_lo[:, k, :], in0=q_ps[k], scalar=qkv_bias[:, 0, k:k + 1],
                    in1=q_hi[:, k, :].bitcast(FP32), op0=ALU.add, op1=ALU.subtract).then_inc(q_lo_done, 1)

            dve.wait_ge(consts, 2)
            pair_stats(0)
            pair_variances(0)
            pair_norm(0)
            dve.wait_ge(qkv_in, 48)
            dve.wait_ge(small_in, 128)
            for n in range(3):
                for k in range(KT):
                    dve.wait_ge(w_hi, n * KT + k + 1)
                    nc.vector.scalar_tensor_tensor(
                        out=wqkv_lo[:, n, k, :], in0=qkv_raw[:, n, k, :], scalar=ln_cols[:, 0, k:k + 1],
                        in1=wqkv_hi[:, n, k, :].bitcast(FP32), op0=ALU.mult, op1=ALU.subtract).then_inc(w_lo, 1)
            dve.wait_ge(bias_mm, 1)
            bias_ps = bank[7]
            nc.vector.tensor_tensor(qkv_bias[:, :, :], bias_ps[:, 0:3 * KT].rearrange("p (n k) -> p n k", n=3),
                                    bias_cols[:, :, :], ALU.add).then_inc(bias_done, 1)
            lower_half(0, 0)
            dve.wait_ge(bias_done, 1)
            for k in range(KT):
                last = nc.vector.tensor_scalar(bv_wide[:, k, :], ident[:, :], 0.0, qkv_bias[:, 2, k:k + 1],
                                               ALU.mult, ALU.add)
            last.then_inc(bv_done, 1)
            keys_lo(0)
            pair_stats(1)
            pair_variances(1)
            pair_norm(1)
            lower_half(1, 1)
            queries_lo(0, 0)
            queries_lo(0, 1)
            dve.wait_ge(rows_in, 32)
            dve.wait_ge(bo_mm, 1)
            nc.vector.tensor_tensor(out_bias[:, :], wo_ps, bo_rows[:, :], ALU.add).then_inc(bo_done, 1)
            dve.wait_ge(mlp_in, 32)
            for k in range(KT):
                dve.wait_ge(mlp_hi, k + 1)
                nc.vector.scalar_tensor_tensor(
                    out=w1_lo[:, k, :], in0=w1_raw[:, k, :], scalar=ln_cols[:, 2, k:k + 1],
                    in1=w1_hi[:, k, :].bitcast(FP32), op0=ALU.mult, op1=ALU.subtract).then_inc(mlp_lo, 1)
            dve.wait_ge(mlp_hi, KT + 1)
            nc.vector.tensor_tensor(w2_lo[:, :, :], w2_raw, w2_hi[:, :, :].bitcast(FP32), ALU.subtract)\
                .then_inc(mlp_lo, 1)
            dve.wait_ge(bias_mm, 2)
            nc.vector.tensor_tensor(mlp_bias[:, :], bias_ps[:, 3 * KT:3 * KT + FT], b1_cols[:, :], ALU.add)\
                .then_inc(bias_done, 1)

            def block_stats(t):
                for j in range(BG):
                    nc.vector.bn_stats(stats2[:, j, :], xs[:, BG * t + j, :]).then_inc(stats2_done, 1)
                for j in range(BG):
                    wait(dve, stats2_done, BG * t + j + 1)
                    apart(dve)
                    nc.vector.bn_aggr(mv2[:, j, :], stats2[:, j, :]).then_inc(mv2_done, 1)
                wait(dve, mv2_done, BG * t + BG)
                nc.vector.tensor_scalar(var_eps2[:, :], mv2[:, :, 1], EPS, None, ALU.add)\
                    .then_inc(var2_done, 1)

            def block_norm(t):
                wait(dve, rstd2_done, t + 1)
                wait(dve, t2_mm, KT * t)
                for j in range(BG):
                    last = nc.vector.tensor_scalar(nx2[:, j, :], xs[:, BG * t + j, :], mv2[:, j, 0:1],
                                                   rstd2[:, j:j + 1], ALU.subtract, ALU.mult)
                last.then_inc(nx2_done, 1)

            def lower_half2(t, par):
                for k in range(KT):
                    wait(dve, n2_hi_done, KT * t + k + 1)
                    nc.vector.tensor_tensor(n2_lo[par][:, k, :], t2_ps[k][:, :],
                                            n2_hi[par][:, k, :].bitcast(FP32), ALU.subtract)\
                        .then_inc(n2_lo_done, 1)

            def halves(t, f):
                u = f % 2
                wait(dve, gelu_done, FT * t + f + 1)
                wait(dve, w2_mm, FT * t + f - 1)
                nc.vector.tensor_copy(h_hi[:, u, :], h_sb[:, u, :]).then_inc(h_hi_done, 1)
                wait(dve, h_hi_done, FT * t + f + 1)
                nc.vector.tensor_tensor(h_lo[:, u, :], h_sb[:, u, :], h_hi[:, u, :].bitcast(FP32),
                                        ALU.subtract).then_inc(h_lo_done, 1)

            def outputs(t):
                wait(dve, w2_mm, FT * t + FT)
                wait(dve, xb2_done, t + 1)
                for j in range(BG):
                    nc.vector.tensor_tensor(xs[:, BG * t + j, :], y_ps[j], xs[:, BG * t + j, :], ALU.add)\
                        .then_inc(y_out, 1)

            def mlp_block(t, par, first, last):
                for f in range(FT):
                    halves(t, f)
                    if f == 0 and not first:
                        outputs(t - 1)
                    if f == 1 and not last:
                        block_stats(t + 1)
                    if f == 2 and not last:
                        block_norm(t + 1)
                    if f == 4 and not last:
                        lower_half2(t + 1, 1 - par)

            def pair(i, par, first, ahead):
                wait(dve, mask_done, i + 1)
                scores(2 * i, 0, 0)
                if not first:
                    residual(i - 1, 2 * i - 2)
                scores(2 * i, 0, 1)
                if not first:
                    weights_out(2 * i - 1)
                reciprocals(2 * i, 0)
                if ahead >= 2:
                    pair_stats(i + 2)
                if ahead >= 1:
                    keys_lo(i + 1)
                if not first:
                    heads_out(2 * i - 1)
                if ahead == 0:
                    block_stats(0)
                scores(2 * i + 1, 1, 0)
                reciprocals(2 * i, 1)
                scores(2 * i + 1, 1, 1)
                if not first:
                    residual(i - 1, 2 * i - 1)
                if ahead >= 2:
                    pair_variances(i + 2)
                if ahead == 0:
                    block_norm(0)
                reciprocals(2 * i + 1, 0)
                weights_out(2 * i)
                if ahead >= 2:
                    pair_norm(i + 2)
                heads_out(2 * i)
                if ahead >= 1:
                    queries_lo(i + 1, 0)
                reciprocals(2 * i + 1, 1)
                if ahead >= 2:
                    lower_half(i + 2, par)
                if ahead >= 1:
                    queries_lo(i + 1, 1)

            pair(0, 0, True, 2)
            with nc.vector.Fori(0, (PAIRS - 4) // 2) as u:
                pair(2 * u + 1, 1, False, 2)
                pair(2 * u + 2, 0, False, 2)
            pair(PAIRS - 3, 1, False, 2)
            pair(PAIRS - 2, 0, False, 1)
            pair(PAIRS - 1, 1, False, 0)
            residual(PAIRS - 1, G - 2)
            lower_half2(0, 0)
            weights_out(G - 1)
            heads_out(G - 1)
            residual(PAIRS - 1, G - 1)

            mlp_block(0, 0, True, False)
            with nc.vector.Fori(0, (BLOCKS - 2) // 2) as u:
                mlp_block(2 * u + 1, 1, False, False)
                mlp_block(2 * u + 2, 0, False, False)
            mlp_block(BLOCKS - 1, 1, False, True)
            outputs(BLOCKS - 1)

        @block.tensor
        def _(pe):
            def split_product(dst, hi, lo, rhs_hi, rhs_lo, ks):
                terms = [(a, b, k) for a, b in ((hi, rhs_hi), (hi, rhs_lo), (lo, rhs_hi)) for k in ks]
                for n, (a, b, k) in enumerate(terms):
                    mm = nc.tensor.matmul(dst, a(k), b(k), start=(n == 0), stop=(n == len(terms) - 1))
                return mm

            def transposed(i):
                wait(pe, nx_done, i + 1)
                wait(pe, lo_done, i)
                wait(pe, pt_second, 2 * i - 3)
                for j in range(2):
                    for k in range(KT):
                        mm = nc.tensor.transpose(t_ps[:, k, j * S:(j + 1) * S],
                                                 nx[:, j, k * P:(k + 1) * P], ident[:, :])
                mm.then_inc(t_done, 1)

            def project(n, dst, m, par):
                cols = slice(m * P, (m + 1) * P)
                return split_product(dst[m], lambda k: wqkv_hi[:, n, k, cols],
                                     lambda k: wqkv_lo[:, n, k, cols],
                                     lambda k: nt_hi[par][:, k, :], lambda k: nt_lo[par][:, k, :], range(KT))

            def keys(i, par):
                wait(pe, hi_done, i + 1)
                wait(pe, lo_done, i + 1)
                for m in range(KT):
                    project(1, k_ps, m, par).then_inc(k_mm, 1)

            def queries(i, m, par):
                if m == 0:
                    wait(pe, k_lo_done, KT * i + KT)
                project(0, q_ps, m, par).then_inc(q0_mm if m == 0 else q_mm, 1)

            def values(i, j, par):
                wait(pe, v_out, i)
                toks = slice(j * S, (j + 1) * S)
                split_product(v_ps[:, j, :], lambda k: nt_hi[par][:, k, toks],
                              lambda k: nt_lo[par][:, k, toks], lambda k: wqkv_hi[:, 2, k, :],
                              lambda k: wqkv_lo[:, 2, k, :], range(KT)).then_inc(v_mm, 1)

            def scores(i, g, j, ks):
                toks = slice(j * S, (j + 1) * S)
                wait(pe, kz_in, 16 * HPT * i + 16 * HPT)
                for k in ks:
                    wait(pe, q_hi_done, KT * i + k + 1)
                    wait(pe, q_lo_done, KT * i + k + 1)
                    wait(pe, z_done, HEADS * (g - 1) + HPT * (k + 1))
                    split_product(s_ps[k], lambda k: q_hi[:, k, toks], lambda k: q_lo[:, k, toks],
                                  lambda k: kz[:, 0, k, :, toks], lambda k: kz[:, 1, k, :, toks], [k])\
                        .then_inc(s_mm, 1)

            def weights_transposed(g, k):
                wait(pe, p_done, 2 * g + k + 1)
                wait(pe, (pt_first, pt_second)[k], g)
                for h in range(HPT):
                    mm = nc.tensor.transpose(pt_ps[k][:, h, :], p_sb[:, HPT * k + h, :], ident[:, :])
                mm.then_inc(pt_mm, 1)

            def weighted_values(i, g, j):
                wait(pe, v_out, i + 1)
                wait(pe, pt_first, g + 1)
                wait(pe, pt_second, g + 1)
                wait(pe, x1_done, g)
                for h in range(HEADS):
                    mm = nc.tensor.matmul(o_ps[D * (h % HPT):D * (h % HPT) + D, h // HPT, :],
                                          v_sb[:, j, D * h:D * h + D], pT[:, h, :], start=True, stop=True)
                mm.then_inc(pv_mm, 1)

            def out_projection(g):
                wait(pe, o_out, g + 1)
                for k in range(KT):
                    mm = nc.tensor.matmul(wo_ps, oT[:, k, :], wo_sb[:, k, :], start=(k == 0),
                                          stop=(k == KT - 1))
                mm.then_inc(wo_mm, 1)

            def pair(i, par, first, ahead):
                scores(i, 2 * i, 0, [1])
                if not first:
                    weights_transposed(2 * i - 1, 0)
                if ahead >= 1:
                    wait(pe, lo_done, i + 2)
                if not first:
                    weights_transposed(2 * i - 1, 1)
                if ahead >= 1:
                    keys(i + 1, 1 - par)
                if not first:
                    weighted_values(i - 1, 2 * i - 1, 1)
                scores(i, 2 * i + 1, 1, range(KT))
                if not first:
                    out_projection(2 * i - 1)
                if ahead >= 1:
                    values(i + 1, 0, 1 - par)
                if ahead == 0:
                    transposed2(0)
                weights_transposed(2 * i, 0)
                weights_transposed(2 * i, 1)
                if ahead >= 1:
                    values(i + 1, 1, 1 - par)
                    queries(i + 1, 0, 1 - par)
                weighted_values(i, 2 * i, 0)
                if ahead >= 2:
                    transposed(i + 2)
                if ahead >= 1:
                    queries(i + 1, 1, 1 - par)
                    scores(i + 1, 2 * i + 2, 0, [0])
                out_projection(2 * i)

            pe.wait_ge(consts, 2)
            transposed(0)
            pe.wait_ge(qkv_in, 48)
            pe.wait_ge(small_in, 128)
            bias_ps = bank[7]
            for n in range(3):
                for m in range(KT):
                    for k in range(KT):
                        mm = nc.tensor.matmul(bias_ps[:, n * KT + m:n * KT + m + 1],
                                              qkv_raw[:, n, k, m * P:(m + 1) * P], ln_cols[:, 1, k:k + 1],
                                              start=(k == 0), stop=(k == KT - 1))
            mm.then_inc(bias_mm, 1)
            pe.wait_ge(w_lo, 3 * KT)
            keys(0, 0)
            values(0, 0, 0)
            values(0, 1, 0)
            queries(0, 0, 0)
            queries(0, 1, 0)
            transposed(1)
            pe.wait_ge(wo_in, 16)
            pe.wait_ge(bv_done, 1)
            for k in range(KT):
                mm = nc.tensor.matmul(wo_ps, bv_wide[:, k, :], wo_sb[:, k, :], start=(k == 0), stop=(k == KT - 1))
            mm.then_inc(bo_mm, 1)
            pe.wait_ge(mlp_in, 32)
            pe.wait_ge(bo_done, 1)
            for f in range(FT):
                for k in range(KT):
                    mm = nc.tensor.matmul(bias_ps[:, 3 * KT + f:3 * KT + f + 1], w1_raw[:, k, f * P:(f + 1) * P],
                                          ln_cols[:, 3, k:k + 1], start=(k == 0), stop=(k == KT - 1))
            mm.then_inc(bias_mm, 1)
            def transposed2(t):
                wait(pe, nx2_done, t + 1)
                wait(pe, n2_lo_done, KT * t)
                for k in range(KT):
                    for j in range(BG):
                        mm = nc.tensor.transpose(t2_ps[k][:, j * S:(j + 1) * S],
                                                 nx2[:, j, k * P:(k + 1) * P], ident[:, :])
                    mm.then_inc(t2_mm, 1)

            def up(t, par, f):
                if f == 0:
                    wait(pe, n2_lo_done, KT * t + KT)
                wait(pe, gelu_done, FT * t + f - 1)
                cols = slice(f * P, (f + 1) * P)
                split_product(h_ps[f % 2][:, :], lambda k: w1_hi[:, k, cols], lambda k: w1_lo[:, k, cols],
                              lambda k: n2_hi[par][:, k, :], lambda k: n2_lo[par][:, k, :], range(KT))\
                    .then_inc(w1_mm, 1)

            def down(t, f):
                wait(pe, h_lo_done, FT * t + f + 1)
                u = f % 2
                for j in range(BG):
                    if f == 0:
                        wait(pe, y_out, BG * (t - 1) + j + 1)
                    toks = slice(j * S, (j + 1) * S)
                    for n, (a, b) in enumerate(((h_hi, w2_hi), (h_hi, w2_lo), (h_lo, w2_hi))):
                        mm = nc.tensor.matmul(y_ps[j], a[:, u, toks], b[:, f, :],
                                              start=(f == 0 and n == 0), stop=(f == FT - 1 and n == 2))
                mm.then_inc(w2_mm, 1)

            def mlp_block(t, par, last):
                for f in range(FT):
                    if f > 0:
                        up(t, par, f)
                        down(t, f - 1)
                    if f == 4 and not last:
                        transposed2(t + 1)
                if not last:
                    up(t + 1, 1 - par, 0)
                down(t, FT - 1)

            pe.wait_ge(bias_done, 2)
            scores(0, 0, 0, [0])
            pair(0, 0, True, 2)
            with nc.tensor.Fori(0, (PAIRS - 4) // 2) as u:
                pair(2 * u + 1, 1, False, 2)
                pair(2 * u + 2, 0, False, 2)
            pair(PAIRS - 3, 1, False, 2)
            pair(PAIRS - 2, 0, False, 1)
            pair(PAIRS - 1, 1, False, 0)
            weights_transposed(G - 1, 0)
            weights_transposed(G - 1, 1)
            pe.wait_ge(z_done, HEADS * G)
            up(0, 0, 0)
            weighted_values(PAIRS - 1, G - 1, 1)
            out_projection(G - 1)
            pe.wait_ge(x1_done, G)
            mlp_block(0, 0, False)
            with nc.tensor.Fori(0, (BLOCKS - 2) // 2) as u:
                mlp_block(2 * u + 1, 1, False)
                mlp_block(2 * u + 2, 0, False)
            mlp_block(BLOCKS - 1, 1, True)


def kernel(**inputs):
    import numpy as np
    import concourse.bacc as bacc
    from concourse import mybir
    from concourse.bass_utils import run_bass_kernel_spmd

    def columns(v):
        return np.ascontiguousarray(np.asarray(v).reshape(-1, 128).T)

    def plain(v):
        return np.ascontiguousarray(np.asarray(v))

    pre = "L0_gnn_"
    arrays = {
        "x": plain(inputs["x"]),
        "adj": np.ascontiguousarray(np.asarray(inputs["adj"]).transpose(1, 0, 2)),
    }
    for n in ("ln1_g", "ln1_b", "ln2_g", "ln2_b"):
        arrays[n] = columns(inputs[pre + n])
    for n in ("q", "k", "v", "o"):
        arrays["w" + n] = plain(inputs[pre + "W" + n])
        arrays["b" + n] = (plain if n == "o" else columns)(inputs[pre + "b" + n])
    for n in ("1", "2"):
        arrays["w" + n] = plain(inputs[pre + "W" + n])
        arrays["b" + n] = (plain if n == "2" else columns)(inputs[pre + "b" + n])

    nc = bacc.Bacc("TRN2", target_bir_lowering=False, num_devices=1)
    aps = {n: nc.dram_tensor(f"in_{n}", a.shape, mybir.dt.from_np(a.dtype), kind="ExternalInput").ap()
           for n, a in arrays.items()}
    out = nc.dram_tensor("out", arrays["x"].shape, mybir.dt.float32, kind="ExternalOutput").ap()
    build_gnn_layer(nc, out=out, **aps)
    r = run_bass_kernel_spmd(nc, [{f"in_{n}": a for n, a in arrays.items()}], core_ids=[0])
    return r.results[0]["out"]
```

```python
import concourse.bass as bass
from concourse import mybir
from contextlib import ExitStack

FP32 = mybir.dt.float32
F32R = mybir.dt.float32r
U8 = mybir.dt.uint8
ALU = mybir.AluOpType
ACT = mybir.ActivationFunctionType

P = 128
EPS = 1e-5
MASKED = 1e30


def build_gnn_layer(nc, x, adj, columns, wq, wk, wv, wo, bo, w1, w2, b2, out):
    G, S, H = x.shape
    HEADS = 8
    D = H // HEADS
    FF = w1.shape[1]
    KT = H // P
    HPT = P // D
    FT = FF // P
    PAIRS = G // 2
    T2 = 2 * S
    BG = 4
    TB = BG * S
    BLOCKS = G // BG
    SCALE = float(D) ** -0.5
    Q, K, V, MLP = range(4)
    assert S == P and H == 2 * P and HPT == 4 and FT == 8

    ctx = ExitStack()
    with ctx:
        def sb(name, shape, dt=FP32):
            return ctx.enter_context(nc.sbuf_tensor(name, shape, dt))

        def sem(name):
            return ctx.enter_context(nc.semaphore(name))

        xs = sb("xs", [P, G, H])
        adj_u8 = sb("adj_u8", [P, 2, S], U8)
        first_f32 = sb("first_f32", [P, 3 * KT * H])
        qkv_raw = first_f32[:, :].rearrange("p (n k c) -> p n k c", n=3, k=KT)
        wqkv_hi = sb("wqkv_hi", [P, 3, KT, H], F32R)
        wqkv_lo = sb("wqkv_lo", [P, 3, KT, H], F32R)
        wo_sb = sb("wo_sb", [P, KT, H])
        w1_hi = sb("w1_hi", [P, KT, FF], F32R)
        w1_lo = sb("w1_lo", [P, KT, FF], F32R)
        w2_hi = sb("w2_hi", [P, FT, H], F32R)
        w2_lo = sb("w2_lo", [P, FT, H], F32R)
        GW = FF * KT // H
        LATE = (G - 2 * GW) // 2
        w1_raw = xs[:, G - 2 * GW:G - GW, :].rearrange("p (k g) c -> p k (g c)", k=KT)
        w2_raw = xs[:, G - GW:G, :]
        cols = sb("cols", [P, 7 * KT + FT])
        ln_cols = cols[:, 0:4 * KT].rearrange("p (n k) -> p n k", n=4)
        bias_cols = cols[:, 4 * KT:7 * KT].rearrange("p (n k) -> p n k", n=3)
        b1_cols = cols[:, 7 * KT:]
        qkv_bias = sb("qkv_bias", [P, 3, KT])
        mlp_bias = sb("mlp_bias", [P, FT])
        bv_wide = sb("bv_wide", [P, KT, P])
        bo_rows = sb("bo_rows", [P, H])
        b2_rows = sb("b2_rows", [P, H])
        out_bias = sb("out_bias", [P, H])
        ident = sb("ident", [P, P])
        minus_half = sb("minus_half", [P, BG])

        stats = sb("stats", [P, 2, 6])
        mv = sb("mv", [P, 2, 2])
        var_eps = sb("var_eps", [P, 2])
        rstd = sb("rstd", [P, 2])
        nx = sb("nx", [P, 2, H])
        nt_all = sb("nt_all", [P, 2 * 2 * KT * T2], F32R)
        nt = [nt_all[:, par * 2 * KT * T2:(par + 1) * 2 * KT * T2]
              .rearrange("p (u k t) -> p u k t", u=2, k=KT) for par in range(2)]
        nt_hi = [nt[par][:, 0, :, :] for par in range(2)]
        nt_lo = [nt[par][:, 1, :, :] for par in range(2)]
        q_hi = sb("q_hi", [P, KT, T2], F32R)
        q_lo = sb("q_lo", [P, KT, T2], F32R)
        k_halves = sb("k_halves", [P, 2, KT, T2], F32R)
        kz_all = sb("kz_all", [P, 2 * KT * HPT * T2], F32R)
        kz = kz_all[:, :].rearrange("p (u k j t) -> p u k j t", u=2, k=KT, j=HPT)
        v_sb = sb("v_sb", [P, 2, H])
        mask_add = sb("mask_add", [P, 2, S])
        z_all = sb("z_all", [P, HEADS * S])
        z_neg = z_all[:, :].rearrange("p (h k) -> p h k", h=HEADS)
        min_z = sb("min_z", [P, HEADS])
        e_sb = sb("e_sb", [P, HEADS, S])
        sums = sb("sums", [P, HEADS])
        rinv = sb("rinv", [P, HEADS])
        p_sb = sb("p_sb", [P, HEADS, S])
        pT = sb("pT", [P, HEADS, S])
        oT = sb("oT", [P, KT, S])

        stats2 = sb("stats2", [P, BG, 6])
        mv2 = sb("mv2", [P, BG, 2])
        var_eps2 = sb("var_eps2", [P, BG])
        rstd2 = sb("rstd2", [P, BG])
        nx2 = first_f32[:, 0:BG * H].rearrange("p (g c) -> p g c", g=BG)
        h_sb = z_all[:, :].rearrange("p (u t) -> p u t", u=2)
        n2_even = nt_all[:, :].rearrange("p (u k t) -> p u k t", u=2, k=KT)
        part = 2 * KT * TB
        n2_odd = kz_all[:, 0:part].rearrange("p (u k t) -> p u k t", u=2, k=KT)
        h_hi = kz_all[:, part:part + 2 * TB].rearrange("p (u t) -> p u t", u=2)
        h_lo = kz_all[:, part + 2 * TB:part + 4 * TB].rearrange("p (u t) -> p u t", u=2)
        n2_hi = [n2_even[:, 0, :, :], n2_odd[:, 0, :, :]]
        n2_lo = [n2_even[:, 1, :, :], n2_odd[:, 1, :, :]]

        bank = [ctx.enter_context(nc.psum_tensor(f"bank{n}", [P, 512], FP32)) for n in range(8)]
        bias_ps = [bank[n][:, 0:KT] for n in (3, 4, 7)] + [bank[5][:, 0:FT]]
        t_ps = bank[6][:, :].rearrange("p (k t) -> p k t", k=KT)
        k_ps = [bank[1][:, 0:T2], bank[0][:, 0:T2]]
        q_ps = [bank[0][:, 0:T2], bank[1][:, 0:T2]]
        v_ps = bank[2][:, :].rearrange("p (g c) -> p g c", g=2)
        s_ps = [bank[3 + k][:, :].rearrange("p (h k) -> p h k", h=HPT) for k in range(KT)]
        pt_ps = [bank[5 + k][:, :].rearrange("p (h q) -> p h q", h=HPT) for k in range(KT)]
        o_ps = bank[7][:, 0:H].rearrange("p (k q) -> p k q", k=KT)
        wo_ps = bank[7][:, H:2 * H]
        t2_ps = [bank[k] for k in range(KT)]
        h_ps = [bank[2], bank[3]]
        y_ps = [bank[4 + j][:, 0:H] for j in range(BG)]

        wait_taken = sem("wait_taken")
        sp_wait_taken = sem("sp_wait_taken")
        pool_wait_taken = sem("pool_wait_taken")
        x_in = sem("x_in")
        adj_in = sem("adj_in")
        qkv_in = [sem("wq_in"), sem("wk_in"), sem("wv_in")]
        cols_in = sem("cols_in")
        rows_in = sem("rows_in")
        wo_in = sem("wo_in")
        w1_in = sem("w1_in")
        w2_in = sem("w2_in")
        out_done = sem("out_done")
        id_zero = sem("id_zero")
        consts = sem("consts")
        kz_zero = sem("kz_zero")
        w_hi = [sem("wq_hi_done"), sem("wk_hi_done"), sem("wv_hi_done")]
        w_lo = [sem("wq_lo_done"), sem("wk_lo_done"), sem("wv_lo_done")]
        mlp_hi = sem("mlp_hi")
        mlp_lo = sem("mlp_lo")
        bias_mm = [sem("bias_q_mm"), sem("bias_k_mm"), sem("bias_v_mm"), sem("bias_mlp_mm")]
        bias_done = [sem("bias_q_done"), sem("bias_k_done"), sem("bias_v_done"), sem("bias_mlp_done")]
        bv_done = sem("bv_done")
        bo_mm = sem("bo_mm")
        bo_done = sem("bo_done")

        stats_done = sem("stats_done")
        mv_done = sem("mv_done")
        var_done = sem("var_done")
        rstd_done = sem("rstd_done")
        nx_done = sem("nx_done")
        mask_done = sem("mask_done")
        xb_done = sem("xb_done")
        t_done = sem("t_done")
        hi_done = sem("hi_done")
        lo_done = sem("lo_done")
        k_mm = sem("k_mm")
        q0_mm = sem("q0_mm")
        q_mm = sem("q_mm")
        v_mm = sem("v_mm")
        k_hi_done = sem("k_hi_done")
        k_lo_done = sem("k_lo_done")
        kz_in = sem("kz_in")
        q_hi_done = sem("q_hi_done")
        q_lo_done = sem("q_lo_done")
        v_out = sem("v_out")
        s_mm = sem("s_mm")
        z_done = sem("z_done")
        e_done = sem("e_done")
        rinv_done = sem("rinv_done")
        p_done = sem("p_done")
        pt_mm = sem("pt_mm")
        pt_first = sem("pt_first")
        pt_second = sem("pt_second")
        pv_mm = sem("pv_mm")
        o_out = sem("o_out")
        wo_mm = sem("wo_mm")
        x1_done = sem("x1_done")

        stats2_done = sem("stats2_done")
        mv2_done = sem("mv2_done")
        var2_done = sem("var2_done")
        rstd2_done = sem("rstd2_done")
        nx2_done = sem("nx2_done")
        xb2_done = sem("xb2_done")
        t2_mm = sem("t2_mm")
        n2_hi_done = sem("n2_hi_done")
        n2_lo_done = sem("n2_lo_done")
        w1_mm = sem("w1_mm")
        gelu_done = sem("gelu_done")
        h_hi_done = sem("h_hi_done")
        h_lo_done = sem("h_lo_done")
        w2_mm = sem("w2_mm")
        y_out = sem("y_out")

        def wait(eng, s, value):
            if not isinstance(value, int) or value > 0:
                eng.wait_ge(s, value)

        def apart(dve):
            dve.sem_inc(wait_taken, 1)

        block = ctx.enter_context(nc.Block())

        @block.sync
        def _(sp):
            x_pairs = x.rearrange("g p c -> p g c")
            out_blocks = out.rearrange("g p c -> p g c")

            def load_pair(i):
                wait(sp, x_in, 16 * i)
                sp.dma_start(xs[:, bass.ts(i, 2), :], x_pairs[:, bass.ts(i, 2), :]).then_inc(x_in, 16)

            def load_edges(i):
                wait(sp, mask_done, i)
                sp.dma_start(adj_u8[:, :, :], adj[:, bass.ts(i, 2), :]).then_inc(adj_in, 16)

            def spread_keys(i):
                wait(sp, k_lo_done, KT * i + KT)
                sp.sem_inc(sp_wait_taken, 1)
                wait(sp, s_mm, 4 * i)
                for j in range(HPT):
                    q = slice(D * j, D * j + D)
                    sp.dma_start(kz[q, :, :, j, :].rearrange("p u k t -> p (u k) t").bitcast(FP32),
                                 k_halves[q, :, :, :].rearrange("p u k t -> p (u k) t").bitcast(FP32))\
                        .then_inc(kz_in, 16)

            load_pair(0)
            load_edges(0)
            load_pair(1)
            sp.dma_start(wo_sb[:, :, :], wo.rearrange("(k p) n -> p k n", p=P)).then_inc(wo_in, 16)
            sp.dma_start(w1_raw, w1.rearrange("(k p) n -> p k n", p=P)).then_inc(w1_in, 16)
            sp.dma_start(w2_raw, w2.rearrange("(f p) n -> p f n", p=P)).then_inc(w2_in, 16)
            load_pair(2)
            sp.wait_ge(kz_zero, 1)
            load_edges(1)
            spread_keys(0)
            with nc.sync.Fori(3, LATE) as i:
                spread_keys(i - 2)
                load_pair(i)
                load_edges(i - 1)
            sp.wait_ge(mlp_lo, KT + 1)
            sp.wait_ge(bias_mm[MLP], FT)
            with nc.sync.Fori(LATE, PAIRS) as i:
                spread_keys(i - 2)
                load_pair(i)
                load_edges(i - 1)
            spread_keys(PAIRS - 2)
            load_edges(PAIRS - 1)
            spread_keys(PAIRS - 1)
            with nc.sync.Fori(0, BLOCKS - 1) as t:
                sp.wait_ge(y_out, BG * t + BG)
                sp.dma_start(out_blocks[:, bass.ts(t, BG), :], xs[:, bass.ts(t, BG), :])\
                    .then_inc(out_done, 16)
            for half in range(2):
                g = G - BG + half * BG // 2
                sp.wait_ge(y_out, g + BG // 2)
                sp.dma_start(out_blocks[:, g:g + BG // 2, :], xs[:, g:g + BG // 2, :]).then_inc(out_done, 16)
            sp.wait_ge(out_done, 16 * (BLOCKS + 1))

        @block.gpsimd
        def _(pool):
            nc.gpsimd.memset(ident[:, :], 0.0).then_inc(id_zero, 1)
            pool.wait_ge(id_zero, 1)
            nc.gpsimd.affine_select(out=ident[:, :], in_=ident[:, :], compare_op=ALU.not_equal,
                                    fill=1.0, base=0, pattern=[[-1, P]], channel_multiplier=1)\
                .then_inc(consts, 1)
            nc.gpsimd.memset(minus_half[:, :], -0.5).then_inc(consts, 1)
            pool.wait_ge(consts, 2)
            for n, row in enumerate((bo, b2)):
                dst = (bo_rows, b2_rows)[n]
                nc.gpsimd.dma_start(dst[:, :], row.partition_broadcast(P)).then_inc(rows_in, 16)

            def inv_std(i):
                wait(pool, var_done, i + 1)
                wait(pool, nx_done, i)
                nc.gpsimd.tensor_tensor(rstd[:, :], var_eps[:, :], minus_half[:, 0:2], ALU.pow)\
                    .then_inc(rstd_done, 1)

            def normalise(g, k):
                wait(pool, rinv_done, 2 * g + k + 1)
                wait(pool, pt_mm, 2 * g - 1 + k)
                hs = slice(HPT * k, HPT * k + HPT)
                nc.gpsimd.tensor_tensor(p_sb[:, hs, :], e_sb[:, hs, :],
                                        rinv[:, hs].unsqueeze(2).to_broadcast([P, HPT, S]),
                                        ALU.mult).then_inc(p_done, 1)

            def add_out_bias(i):
                wait(pool, nx_done, i + 1)
                nc.gpsimd.tensor_tensor(xs[:, bass.ts(i, 2), :], xs[:, bass.ts(i, 2), :],
                                        out_bias[:, :].unsqueeze(1).to_broadcast([P, 2, H]),
                                        ALU.add).then_inc(xb_done, 1)

            def inv_std2(t):
                wait(pool, var2_done, t + 1)
                nc.gpsimd.tensor_tensor(rstd2[:, :], var_eps2[:, :], minus_half[:, :], ALU.pow)\
                    .then_inc(rstd2_done, 1)

            def masks(i):
                wait(pool, adj_in, 16 * i + 16)
                wait(pool, z_done, 2 * HEADS * i)
                pool.sem_inc(pool_wait_taken, 1)
                nc.gpsimd.tensor_scalar(mask_add[:, :, :], adj_u8[:, :, :], MASKED, -MASKED, ALU.mult,
                                        ALU.add).then_inc(mask_done, 1)

            def pair(i, ahead):
                normalise(2 * i, 0)
                normalise(2 * i, 1)
                if ahead >= 2:
                    inv_std(i + 2)
                if ahead == 1:
                    inv_std2(0)
                if ahead >= 1:
                    masks(i + 1)
                normalise(2 * i + 1, 0)
                normalise(2 * i + 1, 1)
                if ahead >= 1:
                    add_out_bias(i + 1)

            inv_std(0)
            masks(0)
            inv_std(1)
            pool.wait_ge(bo_done, 1)
            add_out_bias(0)
            pair(0, 2)
            with nc.gpsimd.Fori(1, PAIRS - 2) as i:
                pair(i, 2)
            pair(PAIRS - 2, 1)
            pair(PAIRS - 1, 0)

            def add_mlp_bias(t):
                wait(pool, nx2_done, t + 1)
                nc.gpsimd.tensor_tensor(xs[:, bass.ts(t, BG), :], xs[:, bass.ts(t, BG), :],
                                        b2_rows[:, :].unsqueeze(1).to_broadcast([P, BG, H]),
                                        ALU.add).then_inc(xb2_done, 1)

            add_mlp_bias(0)
            with nc.gpsimd.Fori(1, BLOCKS) as t:
                inv_std2(t)
                add_mlp_bias(t)

        @block.scalar
        def _(act):
            act.dma_start(cols[:, :], columns).then_inc(cols_in, 16)
            for n in (K, V, Q):
                act.dma_start(qkv_raw[:, n, :, :], (wq, wk, wv)[n].rearrange("(k p) n -> p k n", p=P))\
                    .then_inc(qkv_in[n], 16)

            def weights_hi(n):
                act.wait_ge(qkv_in[n], 16)
                act.wait_ge(cols_in, 16)
                for k in range(KT):
                    nc.scalar.activation(wqkv_hi[:, n, k, :], qkv_raw[:, n, k, :], ACT.Copy,
                                         scale=ln_cols[:, 0, k:k + 1]).then_inc(w_hi[n], 1)

            def upper_half(i, par):
                wait(act, t_done, i + 1)
                wait(act, q_mm, i - 1)
                nc.scalar.activation(nt_hi[par], t_ps, ACT.Copy).then_inc(hi_done, 1)

            def keys_hi(i):
                wait(act, kz_in, 16 * HPT * i)
                for k in range(KT):
                    wait(act, k_mm, KT * i + k + 1)
                    nc.scalar.activation(k_halves[:, 0, k, :], k_ps[k], ACT.Identity,
                                         bias=qkv_bias[:, K, k:k + 1]).then_inc(k_hi_done, 1)

            def queries_hi(i, k):
                wait(act, q0_mm if k == 0 else q_mm, i + 1)
                wait(act, s_mm, 4 * i)
                nc.scalar.activation(q_hi[:, k, :], q_ps[k], ACT.Identity,
                                     bias=qkv_bias[:, Q, k:k + 1]).then_inc(q_hi_done, 1)

            def values(i):
                wait(act, v_mm, 2 * i + 2)
                wait(act, pv_mm, 2 * i)
                nc.scalar.activation(v_sb[:, :, :], v_ps, ACT.Copy).then_inc(v_out, 1)

            def exps(g, heads):
                for h in heads:
                    wait(act, z_done, HEADS * g + h + 1)
                    if h % HPT == 0:
                        wait(act, p_done, 2 * g - 1 + h // HPT)
                    nc.scalar.activation(e_sb[:, h, :], z_neg[:, h, :], ACT.Exp,
                                         bias=min_z[:, h:h + 1], scale=-1.0,
                                         accum_out=sums[:, h:h + 1]).then_inc(e_done, 1)

            def weights_out(g):
                wait(act, pt_mm, 2 * g + 1)
                wait(act, pv_mm, g)
                nc.scalar.activation(pT[:, 0:HPT, :], pt_ps[0], ACT.Copy).then_inc(pt_first, 1)

            def pair(i, par, first, ahead):
                exps(2 * i, range(0, 4))
                if not first:
                    weights_out(2 * i - 1)
                exps(2 * i, range(4, 5))
                if ahead >= 1:
                    keys_hi(i + 1)
                if ahead == 0:
                    upper_half2(0, 0)
                exps(2 * i, range(5, 6))
                values(i)
                exps(2 * i, range(6, HEADS))
                exps(2 * i + 1, range(0, 4))
                weights_out(2 * i)
                exps(2 * i + 1, range(4, 7))
                if ahead >= 1:
                    queries_hi(i + 1, 0)
                exps(2 * i + 1, range(7, HEADS))
                if ahead >= 2:
                    upper_half(i + 2, par)
                if ahead >= 1:
                    queries_hi(i + 1, 1)

            def upper_half2(t, par):
                for k in range(KT):
                    wait(act, t2_mm, KT * t + k + 1)
                    wait(act, w1_mm, FT * (t - 1))
                    nc.scalar.activation(n2_hi[par][:, k, :], t2_ps[k][:, :], ACT.Copy)\
                        .then_inc(n2_hi_done, 1)

            def w1_upper():
                act.wait_ge(w1_in, 16)
                for k in range(KT):
                    nc.scalar.activation(w1_hi[:, k, :], w1_raw[:, k, :], ACT.Copy,
                                         scale=ln_cols[:, 2, k:k + 1]).then_inc(mlp_hi, 1)

            def w2_upper():
                act.wait_ge(w2_in, 16)
                nc.scalar.activation(w2_hi[:, :, :], w2_raw, ACT.Copy).then_inc(mlp_hi, 1)

            weights_hi(K)
            weights_hi(V)
            upper_half(0, 0)
            weights_hi(Q)
            act.wait_ge(bias_done[K], 1)
            keys_hi(0)
            w1_upper()
            act.wait_ge(bias_done[Q], 1)
            queries_hi(0, 0)
            queries_hi(0, 1)
            upper_half(1, 1)
            w2_upper()
            pair(0, 0, True, 2)
            with nc.scalar.Fori(0, (PAIRS - 4) // 2) as u:
                pair(2 * u + 1, 1, False, 2)
                pair(2 * u + 2, 0, False, 2)
            pair(PAIRS - 3, 1, False, 2)
            pair(PAIRS - 2, 0, False, 1)
            pair(PAIRS - 1, 1, False, 0)
            weights_out(G - 1)

            def gelu(t, f):
                wait(act, w1_mm, FT * t + f + 1)
                wait(act, h_lo_done, FT * t + f - 1)
                nc.scalar.activation(h_sb[:, f % 2, :], h_ps[f % 2][:, :], ACT.Gelu,
                                     bias=mlp_bias[:, f:f + 1]).then_inc(gelu_done, 1)

            def mlp_block(t, par, last):
                for f in range(FT):
                    gelu(t, f)
                    if f == 4 and not last:
                        upper_half2(t + 1, 1 - par)

            act.wait_ge(e_done, HEADS * G)
            mlp_block(0, 0, False)
            with nc.scalar.Fori(0, (BLOCKS - 2) // 2) as u:
                mlp_block(2 * u + 1, 1, False)
                mlp_block(2 * u + 2, 0, False)
            mlp_block(BLOCKS - 1, 1, True)

        @block.vector
        def _(dve):
            nc.vector.memset(kz_all[:, :].bitcast(FP32), 0.0).then_inc(kz_zero, 1)

            def pair_stats(i):
                wait(dve, x_in, 16 * i + 16)
                for j in range(2):
                    nc.vector.bn_stats(stats[:, j, :], xs[:, 2 * i + j, :]).then_inc(stats_done, 1)

            def pair_variances(i):
                for j in range(2):
                    wait(dve, stats_done, 2 * i + j + 1)
                    apart(dve)
                    nc.vector.bn_aggr(mv[:, j, :], stats[:, j, :]).then_inc(mv_done, 1)
                wait(dve, mv_done, 2 * i + 2)
                wait(dve, rstd_done, i)
                nc.vector.tensor_scalar(var_eps[:, :], mv[:, :, 1], EPS, None, ALU.add)\
                    .then_inc(var_done, 1)

            def pair_norm(i):
                wait(dve, rstd_done, i + 1)
                wait(dve, t_done, i)
                for j in range(2):
                    last = nc.vector.tensor_scalar(nx[:, j, :], xs[:, 2 * i + j, :], mv[:, j, 0:1],
                                                   rstd[:, j:j + 1], ALU.subtract, ALU.mult)
                last.then_inc(nx_done, 1)

            def scores(g, j, k):
                wait(dve, e_done, HEADS * (g - 1) + HPT * (k + 1))
                wait(dve, s_mm, 2 * g + k + 1)
                apart(dve)
                for h in range(HPT * k, HPT * k + HPT):
                    nc.vector.tensor_tensor_reduce(
                        out=z_neg[:, h, :], in0=s_ps[h // HPT][:, h % HPT, :], in1=mask_add[:, j, :],
                        scale=-SCALE, scalar=3e38, op0=ALU.add, op1=ALU.min,
                        accum_out=min_z[:, h:h + 1]).then_inc(z_done, 1)

            def reciprocals(g, k):
                wait(dve, e_done, HEADS * g + HPT * (k + 1))
                hs = slice(HPT * k, HPT * k + HPT)
                nc.vector.reciprocal(rinv[:, hs], sums[:, hs]).then_inc(rinv_done, 1)

            def weights_out(g):
                wait(dve, pt_mm, 2 * g + 2)
                wait(dve, pv_mm, g)
                nc.vector.tensor_copy(pT[:, HPT:HEADS, :], pt_ps[1]).then_inc(pt_second, 1)

            def heads_out(g):
                wait(dve, pv_mm, g + 1)
                wait(dve, wo_mm, g)
                nc.vector.tensor_copy(oT[:, :, :], o_ps).then_inc(o_out, 1)

            def residual(i, g):
                wait(dve, wo_mm, g + 1)
                wait(dve, xb_done, i + 1)
                nc.vector.tensor_tensor(xs[:, g, :], wo_ps, xs[:, g, :], ALU.add).then_inc(x1_done, 1)

            def lower_half(i, par):
                wait(dve, hi_done, i + 1)
                wait(dve, q_mm, i - 1)
                nc.vector.tensor_tensor(nt_lo[par], t_ps, nt_hi[par].bitcast(FP32), ALU.subtract)\
                    .then_inc(lo_done, 1)

            def keys_lo(i):
                wait(dve, kz_in, 16 * HPT * i)
                for k in range(KT):
                    wait(dve, k_hi_done, KT * i + k + 1)
                    nc.vector.scalar_tensor_tensor(
                        out=k_halves[:, 1, k, :], in0=k_ps[k], scalar=qkv_bias[:, K, k:k + 1],
                        in1=k_halves[:, 0, k, :].bitcast(FP32), op0=ALU.add, op1=ALU.subtract)\
                        .then_inc(k_lo_done, 1)

            def queries_lo(i, k):
                wait(dve, q_hi_done, KT * i + k + 1)
                wait(dve, s_mm, 4 * i)
                nc.vector.scalar_tensor_tensor(
                    out=q_lo[:, k, :], in0=q_ps[k], scalar=qkv_bias[:, Q, k:k + 1],
                    in1=q_hi[:, k, :].bitcast(FP32), op0=ALU.add, op1=ALU.subtract).then_inc(q_lo_done, 1)

            def weights_lo(n):
                dve.wait_ge(qkv_in[n], 16)
                dve.wait_ge(cols_in, 16)
                for k in range(KT):
                    dve.wait_ge(w_hi[n], k + 1)
                    nc.vector.scalar_tensor_tensor(
                        out=wqkv_lo[:, n, k, :], in0=qkv_raw[:, n, k, :], scalar=ln_cols[:, 0, k:k + 1],
                        in1=wqkv_hi[:, n, k, :].bitcast(FP32), op0=ALU.mult, op1=ALU.subtract).then_inc(w_lo[n], 1)

            def shifted_bias(n):
                dve.wait_ge(bias_mm[n], 1)
                nc.vector.tensor_tensor(qkv_bias[:, n, :], bias_ps[n], bias_cols[:, n, :], ALU.add)\
                    .then_inc(bias_done[n], 1)

            def w1_lower(k):
                dve.wait_ge(w1_in, 16)
                dve.wait_ge(mlp_hi, k + 1)
                nc.vector.scalar_tensor_tensor(
                    out=w1_lo[:, k, :], in0=w1_raw[:, k, :], scalar=ln_cols[:, 2, k:k + 1],
                    in1=w1_hi[:, k, :].bitcast(FP32), op0=ALU.mult, op1=ALU.subtract).then_inc(mlp_lo, 1)

            def w2_lower():
                dve.wait_ge(w2_in, 16)
                dve.wait_ge(mlp_hi, KT + 1)
                nc.vector.tensor_tensor(w2_lo[:, :, :], w2_raw, w2_hi[:, :, :].bitcast(FP32), ALU.subtract)\
                    .then_inc(mlp_lo, 1)

            def shifted_mlp_bias():
                dve.wait_ge(bias_mm[MLP], FT)
                nc.vector.tensor_tensor(mlp_bias[:, :], bias_ps[MLP], b1_cols[:, :], ALU.add)\
                    .then_inc(bias_done[MLP], 1)

            dve.wait_ge(consts, 2)
            pair_stats(0)
            pair_variances(0)
            pair_norm(0)
            weights_lo(K)
            weights_lo(V)
            lower_half(0, 0)
            shifted_bias(K)
            weights_lo(Q)
            shifted_bias(V)
            pair_stats(1)
            pair_variances(1)
            pair_norm(1)
            dve.wait_ge(bias_done[K], 1)
            keys_lo(0)
            dve.wait_ge(bias_done[V], 1)
            for k in range(KT):
                last = nc.vector.tensor_scalar(bv_wide[:, k, :], ident[:, :], 0.0, qkv_bias[:, V, k:k + 1],
                                               ALU.mult, ALU.add)
            last.then_inc(bv_done, 1)
            w1_lower(0)
            shifted_bias(Q)
            w1_lower(1)
            dve.wait_ge(bias_done[Q], 1)
            queries_lo(0, 0)
            queries_lo(0, 1)
            lower_half(1, 1)
            dve.wait_ge(rows_in, 32)
            dve.wait_ge(bo_mm, 1)
            nc.vector.tensor_tensor(out_bias[:, :], wo_ps, bo_rows[:, :], ALU.add).then_inc(bo_done, 1)

            def block_stats(t):
                for j in range(BG):
                    nc.vector.bn_stats(stats2[:, j, :], xs[:, BG * t + j, :]).then_inc(stats2_done, 1)

            def block_variances(t):
                for j in range(BG):
                    wait(dve, stats2_done, BG * t + j + 1)
                    apart(dve)
                    nc.vector.bn_aggr(mv2[:, j, :], stats2[:, j, :]).then_inc(mv2_done, 1)
                wait(dve, mv2_done, BG * t + BG)
                nc.vector.tensor_scalar(var_eps2[:, :], mv2[:, :, 1], EPS, None, ALU.add)\
                    .then_inc(var2_done, 1)

            def block_norm(t):
                wait(dve, rstd2_done, t + 1)
                wait(dve, t2_mm, KT * t)
                for j in range(BG):
                    last = nc.vector.tensor_scalar(nx2[:, j, :], xs[:, BG * t + j, :], mv2[:, j, 0:1],
                                                   rstd2[:, j:j + 1], ALU.subtract, ALU.mult)
                last.then_inc(nx2_done, 1)

            def lower_half2(t, par):
                for k in range(KT):
                    wait(dve, n2_hi_done, KT * t + k + 1)
                    nc.vector.tensor_tensor(n2_lo[par][:, k, :], t2_ps[k][:, :],
                                            n2_hi[par][:, k, :].bitcast(FP32), ALU.subtract)\
                        .then_inc(n2_lo_done, 1)

            def halves(t, f):
                u = f % 2
                wait(dve, gelu_done, FT * t + f + 1)
                wait(dve, w2_mm, FT * t + f - 1)
                nc.vector.tensor_copy(h_hi[:, u, :], h_sb[:, u, :]).then_inc(h_hi_done, 1)
                wait(dve, h_hi_done, FT * t + f + 1)
                nc.vector.tensor_tensor(h_lo[:, u, :], h_sb[:, u, :], h_hi[:, u, :].bitcast(FP32),
                                        ALU.subtract).then_inc(h_lo_done, 1)

            def outputs(t):
                wait(dve, w2_mm, FT * t + FT)
                wait(dve, xb2_done, t + 1)
                for j in range(BG):
                    nc.vector.tensor_tensor(xs[:, BG * t + j, :], y_ps[j], xs[:, BG * t + j, :], ALU.add)\
                        .then_inc(y_out, 1)

            def mlp_block(t, par, first, last):
                for f in range(FT):
                    halves(t, f)
                    if f == 0 and not first:
                        outputs(t - 1)
                    if f == 1 and not last:
                        block_stats(t + 1)
                        block_variances(t + 1)
                    if f == 2 and not last:
                        block_norm(t + 1)
                    if f == 4 and not last:
                        lower_half2(t + 1, 1 - par)

            def pair(i, par, first, ahead):
                wait(dve, mask_done, i + 1)
                scores(2 * i, 0, 0)
                if not first:
                    residual(i - 1, 2 * i - 2)
                scores(2 * i, 0, 1)
                if not first:
                    weights_out(2 * i - 1)
                reciprocals(2 * i, 0)
                if ahead >= 2:
                    pair_stats(i + 2)
                if ahead == 1:
                    block_stats(0)
                if ahead >= 1:
                    keys_lo(i + 1)
                if ahead == 0:
                    lower_half2(0, 0)
                if not first:
                    heads_out(2 * i - 1)
                scores(2 * i + 1, 1, 0)
                reciprocals(2 * i, 1)
                scores(2 * i + 1, 1, 1)
                if first:
                    shifted_mlp_bias()
                if not first:
                    residual(i - 1, 2 * i - 1)
                if ahead >= 2:
                    pair_variances(i + 2)
                if ahead == 1:
                    block_variances(0)
                reciprocals(2 * i + 1, 0)
                if first:
                    w2_lower()
                weights_out(2 * i)
                if ahead >= 2:
                    pair_norm(i + 2)
                if ahead == 1:
                    block_norm(0)
                if ahead >= 1:
                    queries_lo(i + 1, 0)
                heads_out(2 * i)
                reciprocals(2 * i + 1, 1)
                if ahead >= 2:
                    lower_half(i + 2, par)
                if ahead >= 1:
                    queries_lo(i + 1, 1)

            pair(0, 0, True, 2)
            with nc.vector.Fori(0, (PAIRS - 4) // 2) as u:
                pair(2 * u + 1, 1, False, 2)
                pair(2 * u + 2, 0, False, 2)
            pair(PAIRS - 3, 1, False, 2)
            pair(PAIRS - 2, 0, False, 1)
            pair(PAIRS - 1, 1, False, 0)
            residual(PAIRS - 1, G - 2)
            weights_out(G - 1)
            heads_out(G - 1)
            residual(PAIRS - 1, G - 1)

            mlp_block(0, 0, True, False)
            with nc.vector.Fori(0, (BLOCKS - 2) // 2) as u:
                mlp_block(2 * u + 1, 1, False, False)
                mlp_block(2 * u + 2, 0, False, False)
            mlp_block(BLOCKS - 1, 1, False, True)
            outputs(BLOCKS - 1)

        @block.tensor
        def _(pe):
            def split_product(dst, hi, lo, rhs_hi, rhs_lo, ks):
                terms = [(a, b, k) for a, b in ((hi, rhs_hi), (hi, rhs_lo), (lo, rhs_hi)) for k in ks]
                for n, (a, b, k) in enumerate(terms):
                    mm = nc.tensor.matmul(dst, a(k), b(k), start=(n == 0), stop=(n == len(terms) - 1))
                return mm

            def transposed(i):
                wait(pe, nx_done, i + 1)
                wait(pe, lo_done, i)
                wait(pe, pt_second, 2 * i - 3)
                for j in range(2):
                    for k in range(KT):
                        mm = nc.tensor.transpose(t_ps[:, k, j * S:(j + 1) * S],
                                                 nx[:, j, k * P:(k + 1) * P], ident[:, :])
                mm.then_inc(t_done, 1)

            def project(n, dst, m, par):
                outs = slice(m * P, (m + 1) * P)
                return split_product(dst[m], lambda k: wqkv_hi[:, n, k, outs],
                                     lambda k: wqkv_lo[:, n, k, outs],
                                     lambda k: nt_hi[par][:, k, :], lambda k: nt_lo[par][:, k, :], range(KT))

            def keys(i, par):
                wait(pe, hi_done, i + 1)
                wait(pe, lo_done, i + 1)
                for m in range(KT):
                    project(K, k_ps, m, par).then_inc(k_mm, 1)

            def queries(i, m, par):
                if m == 0:
                    wait(pe, k_lo_done, KT * i + KT)
                project(Q, q_ps, m, par).then_inc(q0_mm if m == 0 else q_mm, 1)

            def values(i, j, par):
                wait(pe, v_out, i)
                toks = slice(j * S, (j + 1) * S)
                split_product(v_ps[:, j, :], lambda k: nt_hi[par][:, k, toks],
                              lambda k: nt_lo[par][:, k, toks], lambda k: wqkv_hi[:, V, k, :],
                              lambda k: wqkv_lo[:, V, k, :], range(KT)).then_inc(v_mm, 1)

            def scores(i, g, j, ks):
                toks = slice(j * S, (j + 1) * S)
                wait(pe, kz_in, 16 * HPT * i + 16 * HPT)
                for k in ks:
                    wait(pe, q_hi_done, KT * i + k + 1)
                    wait(pe, q_lo_done, KT * i + k + 1)
                    wait(pe, z_done, HEADS * (g - 1) + HPT * (k + 1))
                    split_product(s_ps[k], lambda k: q_hi[:, k, toks], lambda k: q_lo[:, k, toks],
                                  lambda k: kz[:, 0, k, :, toks], lambda k: kz[:, 1, k, :, toks], [k])\
                        .then_inc(s_mm, 1)

            def weights_transposed(g, k):
                wait(pe, p_done, 2 * g + k + 1)
                wait(pe, (pt_first, pt_second)[k], g)
                for h in range(HPT):
                    mm = nc.tensor.transpose(pt_ps[k][:, h, :], p_sb[:, HPT * k + h, :], ident[:, :])
                mm.then_inc(pt_mm, 1)

            def weighted_values(i, g, j):
                wait(pe, v_out, i + 1)
                wait(pe, pt_first, g + 1)
                wait(pe, pt_second, g + 1)
                wait(pe, x1_done, g)
                for h in range(HEADS):
                    mm = nc.tensor.matmul(o_ps[D * (h % HPT):D * (h % HPT) + D, h // HPT, :],
                                          v_sb[:, j, D * h:D * h + D], pT[:, h, :], start=True, stop=True)
                mm.then_inc(pv_mm, 1)

            def out_projection(g):
                wait(pe, o_out, g + 1)
                for k in range(KT):
                    mm = nc.tensor.matmul(wo_ps, oT[:, k, :], wo_sb[:, k, :], start=(k == 0),
                                          stop=(k == KT - 1))
                mm.then_inc(wo_mm, 1)

            def pair(i, par, first, ahead):
                scores(i, 2 * i, 0, [1])
                if not first:
                    weights_transposed(2 * i - 1, 0)
                if ahead >= 1:
                    wait(pe, lo_done, i + 2)
                if not first:
                    weights_transposed(2 * i - 1, 1)
                if ahead >= 1:
                    keys(i + 1, 1 - par)
                if ahead == 0:
                    transposed2(0)
                if not first:
                    weighted_values(i - 1, 2 * i - 1, 1)
                scores(i, 2 * i + 1, 1, range(KT))
                if not first:
                    out_projection(2 * i - 1)
                if first:
                    mlp_bias_part(range(FT // 2, FT))
                if ahead >= 1:
                    values(i + 1, 0, 1 - par)
                if ahead == 0:
                    pe.wait_ge(v_out, PAIRS)
                    up(0, 0, 0)
                if first:
                    pe.wait_ge(bias_done[MLP], 1)
                    pe.wait_ge(bo_done, 1)
                weights_transposed(2 * i, 0)
                weights_transposed(2 * i, 1)
                if ahead == 0:
                    pe.wait_ge(z_done, HEADS * G - HPT)
                    up(0, 0, 1)
                if ahead >= 1:
                    values(i + 1, 1, 1 - par)
                    queries(i + 1, 0, 1 - par)
                weighted_values(i, 2 * i, 0)
                if ahead >= 2:
                    transposed(i + 2)
                if ahead >= 1:
                    queries(i + 1, 1, 1 - par)
                    scores(i + 1, 2 * i + 2, 0, [0])
                out_projection(2 * i)

            def bias_part(n):
                pe.wait_ge(qkv_in[n], 16)
                pe.wait_ge(cols_in, 16)
                for m in range(KT):
                    for k in range(KT):
                        mm = nc.tensor.matmul(bias_ps[n][:, m:m + 1], qkv_raw[:, n, k, m * P:(m + 1) * P],
                                              ln_cols[:, 1, k:k + 1], start=(k == 0), stop=(k == KT - 1))
                mm.then_inc(bias_mm[n], 1)

            def mlp_bias_part(fs):
                pe.wait_ge(w1_in, 16)
                for f in fs:
                    for k in range(KT):
                        mm = nc.tensor.matmul(bias_ps[MLP][:, f:f + 1], w1_raw[:, k, f * P:(f + 1) * P],
                                              ln_cols[:, 3, k:k + 1], start=(k == 0), stop=(k == KT - 1))
                    mm.then_inc(bias_mm[MLP], 1)

            bias_part(K)
            pe.wait_ge(consts, 2)
            transposed(0)
            bias_part(V)
            pe.wait_ge(w_lo[K], KT)
            keys(0, 0)
            pe.wait_ge(w_lo[V], KT)
            values(0, 0, 0)
            values(0, 1, 0)
            bias_part(Q)
            pe.wait_ge(w_lo[Q], KT)
            queries(0, 0, 0)
            queries(0, 1, 0)
            transposed(1)
            pe.wait_ge(wo_in, 16)
            pe.wait_ge(bv_done, 1)
            for k in range(KT):
                mm = nc.tensor.matmul(wo_ps, bv_wide[:, k, :], wo_sb[:, k, :], start=(k == 0), stop=(k == KT - 1))
            mm.then_inc(bo_mm, 1)
            mlp_bias_part(range(FT // 2))

            def transposed2(t):
                wait(pe, nx2_done, t + 1)
                wait(pe, n2_lo_done, KT * t)
                for k in range(KT):
                    for j in range(BG):
                        mm = nc.tensor.transpose(t2_ps[k][:, j * S:(j + 1) * S],
                                                 nx2[:, j, k * P:(k + 1) * P], ident[:, :])
                    mm.then_inc(t2_mm, 1)

            def up(t, par, f):
                if f == 0:
                    wait(pe, n2_lo_done, KT * t + KT)
                wait(pe, gelu_done, FT * t + f - 1)
                outs = slice(f * P, (f + 1) * P)
                split_product(h_ps[f % 2][:, :], lambda k: w1_hi[:, k, outs], lambda k: w1_lo[:, k, outs],
                              lambda k: n2_hi[par][:, k, :], lambda k: n2_lo[par][:, k, :], range(KT))\
                    .then_inc(w1_mm, 1)

            def down(t, f):
                wait(pe, h_lo_done, FT * t + f + 1)
                u = f % 2
                for j in range(BG):
                    if f == 0:
                        wait(pe, y_out, BG * (t - 1) + j + 1)
                    toks = slice(j * S, (j + 1) * S)
                    for n, (a, b) in enumerate(((h_hi, w2_hi), (h_hi, w2_lo), (h_lo, w2_hi))):
                        mm = nc.tensor.matmul(y_ps[j], a[:, u, toks], b[:, f, :],
                                              start=(f == 0 and n == 0), stop=(f == FT - 1 and n == 2))
                mm.then_inc(w2_mm, 1)

            def mlp_block(t, par, first, last):
                for f in range(FT):
                    if f > (1 if first else 0):
                        up(t, par, f)
                    if f > 0:
                        down(t, f - 1)
                    if f == 4 and not last:
                        transposed2(t + 1)
                if not last:
                    up(t + 1, 1 - par, 0)
                down(t, FT - 1)

            pe.wait_ge(bias_done[Q], 1)
            pe.wait_ge(bias_done[K], 1)
            scores(0, 0, 0, [0])
            pair(0, 0, True, 2)
            with nc.tensor.Fori(0, (PAIRS - 4) // 2) as u:
                pair(2 * u + 1, 1, False, 2)
                pair(2 * u + 2, 0, False, 2)
            pair(PAIRS - 3, 1, False, 2)
            pair(PAIRS - 2, 0, False, 1)
            pair(PAIRS - 1, 1, False, 0)
            weights_transposed(G - 1, 0)
            weights_transposed(G - 1, 1)
            weighted_values(PAIRS - 1, G - 1, 1)
            out_projection(G - 1)
            pe.wait_ge(z_done, HEADS * G)
            pe.wait_ge(x1_done, G)
            mlp_block(0, 0, True, False)
            with nc.tensor.Fori(0, (BLOCKS - 2) // 2) as u:
                mlp_block(2 * u + 1, 1, False, False)
                mlp_block(2 * u + 2, 0, False, False)
            mlp_block(BLOCKS - 1, 1, False, True)


def kernel(**inputs):
    import numpy as np
    import concourse.bacc as bacc
    from concourse import mybir
    from concourse.bass_utils import run_bass_kernel_spmd

    def columns(v):
        return np.ascontiguousarray(np.asarray(v).reshape(-1, 128).T)

    def plain(v):
        return np.ascontiguousarray(np.asarray(v))

    pre = "L0_gnn_"
    vectors = ("ln1_g", "ln1_b", "ln2_g", "ln2_b", "bq", "bk", "bv", "b1")
    arrays = {
        "x": plain(inputs["x"]),
        "adj": np.ascontiguousarray(np.asarray(inputs["adj"]).transpose(1, 0, 2)),
        "columns": plain(np.concatenate([columns(inputs[pre + n]) for n in vectors], axis=1)),
    }
    for n in ("Wq", "Wk", "Wv", "Wo", "bo", "W1", "W2", "b2"):
        arrays[n.lower()] = plain(inputs[pre + n])

    nc = bacc.Bacc("TRN2", target_bir_lowering=False, num_devices=1)
    aps = {n: nc.dram_tensor(f"in_{n}", a.shape, mybir.dt.from_np(a.dtype), kind="ExternalInput").ap()
           for n, a in arrays.items()}
    out = nc.dram_tensor("out", arrays["x"].shape, mybir.dt.float32, kind="ExternalOutput").ap()
    build_gnn_layer(nc, out=out, **aps)
    r = run_bass_kernel_spmd(nc, [{f"in_{n}": a for n, a in arrays.items()}], core_ids=[0])
    return r.results[0]["out"]
```
